# Optimizing a Trainium2 kernel written in Bass

```python
import numpy as np
import jax
import jax.numpy as jnp

def _softmax(x, axis=-1):
    return jax.nn.softmax(x, axis=axis)

def _gelu(x):
    return jax.nn.gelu(x, approximate=True)

def _silu(x):
    return jax.nn.silu(x)

def _sigmoid(x):
    return jax.nn.sigmoid(x)

def _layernorm(x, axis=-1, eps=1e-05):
    m = jnp.mean(x, axis=axis, keepdims=True)
    v = jnp.var(x, axis=axis, keepdims=True)
    return (x - m) / jnp.sqrt(v + eps)

def _scatter_add(tgt, idx, src, axis=0):
    return tgt.at[idx].add(src)

def _segment_sum(src, seg, n):
    return jax.ops.segment_sum(src, seg, n)
kernel_name = 'mk_macaron_d1_jaxref_r4_8e966c'

def setup_inputs(seed: int=0):
    np.random.seed(seed)
    _w = jnp.asarray

    def _L0_attn_setup():
        import jax, jax.numpy as jnp
        import numpy as np
        B, S, D, H = (4, 512, 256, 16)
        DK = D // H
        key = jax.random.key(seed)
        ks = jax.random.split(key, 5)
        scale = 1.0 / np.sqrt(D)
        x = jax.random.normal(ks[0], (B, S, D), dtype=jnp.float32)
        w_q = jax.random.normal(ks[1], (D, D), dtype=jnp.float32) * scale
        w_k = jax.random.normal(ks[2], (D, D), dtype=jnp.float32) * scale
        w_v = jax.random.normal(ks[3], (D, D), dtype=jnp.float32) * scale
        w_o = jax.random.normal(ks[4], (D, D), dtype=jnp.float32) * scale
        b_o = jnp.zeros((D,), dtype=jnp.float32)
        return {'x': x, 'w_q': w_q, 'w_k': w_k, 'w_v': w_v, 'w_o': w_o, 'b_o': b_o}
    _L0_attn_in = _L0_attn_setup()

    def _L0_ffn_setup():
        import jax, jax.numpy as jnp
        import numpy as np
        import math
        D_IN = 256
        FEATURES = (1024, 1024, 256)
        BATCH, SEQ = (8, 512)

        def _conn_dense(kernel_bool, x):
            w = jnp.where(kernel_bool, jnp.float32(1.0), jnp.float32(-1.0))
            return x @ w
        key = jax.random.key(seed)
        kx, kk0, kk1, kk2 = jax.random.split(key, 4)
        x = jax.random.normal(kx, (BATCH, SEQ, D_IN), dtype=jnp.float32)
        k0 = jax.random.randint(kk0, (2 * D_IN, FEATURES[0]), 0, 2).astype(jnp.bool_)
        k1 = jax.random.randint(kk1, (FEATURES[0], FEATURES[1]), 0, 2).astype(jnp.bool_)
        k2 = jax.random.randint(kk2, (FEATURES[1], FEATURES[2]), 0, 2).astype(jnp.bool_)
        s0 = jnp.asarray(1.0 / math.sqrt(2 * D_IN), dtype=jnp.float32)
        s1 = jnp.asarray(1.0 / math.sqrt(FEATURES[0]), dtype=jnp.float32)
        s2 = jnp.asarray(1.0 / math.sqrt(FEATURES[1]), dtype=jnp.float32)
        return {'x': x, 'k0': k0, 'k1': k1, 'k2': k2, 's0': s0, 's1': s1, 's2': s2}
    _L0_ffn_in = _L0_ffn_setup()
    _d = {'L0_attn_x': _L0_attn_in['x'], 'L0_attn_w_q': _L0_attn_in['w_q'], 'L0_attn_w_k': _L0_attn_in['w_k'], 'L0_attn_w_v': _L0_attn_in['w_v'], 'L0_attn_w_o': _L0_attn_in['w_o'], 'L0_attn_b_o': _L0_attn_in['b_o'], 'L0_ffn_k0': _L0_ffn_in['k0'], 'L0_ffn_k1': _L0_ffn_in['k1'], 'L0_ffn_k2': _L0_ffn_in['k2'], 'L0_ffn_s0': _L0_ffn_in['s0'], 'L0_ffn_s1': _L0_ffn_in['s1'], 'L0_ffn_s2': _L0_ffn_in['s2']}
    _x0 = _d['L0_attn_x']
    _d['L0_attn_x'] = jax.random.normal(jax.random.fold_in(jax.random.key(seed), 1), (2, 2048, 256), dtype=_x0.dtype)
    del _x0
    return _d

def reference(L0_attn_x, L0_attn_w_q, L0_attn_w_k, L0_attn_w_v, L0_attn_w_o, L0_attn_b_o, L0_ffn_k0, L0_ffn_k1, L0_ffn_k2, L0_ffn_s0, L0_ffn_s1, L0_ffn_s2):

    def _L0_attn_ref(x, w_q, w_k, w_v, w_o, b_o):
        import jax, jax.numpy as jnp
        import numpy as np
        B, S, D, H = (4, 512, 256, 16)
        DK = D // H
        b, s, d = x.shape
        q = (x @ w_q.T).reshape(b, s, H, DK).transpose(0, 2, 1, 3)
        k = (x @ w_k.T).reshape(b, s, H, DK).transpose(0, 2, 1, 3)
        v = (x @ w_v.T).reshape(b, s, H, DK).transpose(0, 2, 1, 3)
        scores = jnp.einsum('bhqd,bhkd->bhqk', q, k) / jnp.sqrt(jnp.float32(DK))
        causal = jnp.triu(jnp.ones((s, s), dtype=bool), k=1)
        scores = jnp.where(causal[None, None], jnp.float32(-1000000000.0), scores)
        attn = jax.nn.softmax(scores, axis=-1)
        ctx = jnp.einsum('bhqk,bhkd->bhqd', attn, v)
        ctx = ctx.transpose(0, 2, 1, 3).reshape(b, s, d)
        return ctx @ w_o.T + b_o

    def _L0_ffn_ref(x, k0, k1, k2, s0, s1, s2):
        import jax, jax.numpy as jnp
        import numpy as np
        import math
        D_IN = 256
        FEATURES = (1024, 1024, 256)
        BATCH, SEQ = (8, 512)

        def _conn_dense(kernel_bool, x):
            w = jnp.where(kernel_bool, jnp.float32(1.0), jnp.float32(-1.0))
            return x @ w
        h = jnp.concatenate([x, -x], axis=-1)
        h = s0 * _conn_dense(k0, h)
        h = jax.nn.relu(h) * 2
        h = s1 * _conn_dense(k1, h)
        h = jax.nn.relu(h) * 2
        h = s2 * _conn_dense(k2, h)
        return h
    x = L0_attn_x
    x = x + 0.5 * _L0_ffn_ref(_layernorm(x, axis=-1), L0_ffn_k0, L0_ffn_k1, L0_ffn_k2, L0_ffn_s0, L0_ffn_s1, L0_ffn_s2)
    x = x + _L0_attn_ref(_layernorm(x, axis=-1), L0_attn_w_q, L0_attn_w_k, L0_attn_w_v, L0_attn_w_o, L0_attn_b_o)
    x = x + 0.5 * _L0_ffn_ref(_layernorm(x, axis=-1), L0_ffn_k0, L0_ffn_k1, L0_ffn_k2, L0_ffn_s0, L0_ffn_s1, L0_ffn_s2)
    return x

_drawn_inputs = setup_inputs


def setup_inputs(seed=0):
    import zlib

    import numpy as np

    out = dict(_drawn_inputs(seed))
    spreads = {'L0_attn_b_o': (0.0, 0.1)}
    factors = {}
    for name, (base, spread) in spreads.items():
        noise = np.random.default_rng([zlib.crc32(name.encode()), seed]).standard_normal(out[name].shape)
        drawn = base * np.exp(spread * noise) if base else spread * noise
        out[name] = jnp.asarray(drawn.astype(out[name].dtype))
    for name, factor in factors.items():
        out[name] = (out[name] * factor).astype(out[name].dtype)
    return out
```

```python
from contextlib import ExitStack

import concourse.bass as bass
from concourse import mybir

F32 = mybir.dt.float32
F16 = mybir.dt.float16
U8 = mybir.dt.uint8
U32 = mybir.dt.uint32
ALU = mybir.AluOpType
ACT = mybir.ActivationFunctionType
AX = mybir.AxisListType
RMAX = bass.bass_isa.ReduceOp.max

P = 128
BATCH, SEQ, D = 2, 2048, 256
HEADS, DK = 16, 16
HID = 1024
TOK = BATCH * SEQ
CH = 512
NCH = TOK // CH
TPC = CH // P
DT = D // P
HT = HID // P
EPS = 1e-5

X_SCALE = 2.0 ** 8
W0_SCALE = 2.0 ** -4
W1_SCALE = 2.0 ** -8
FFN_UNSCALE = 1.0 / (X_SCALE * W0_SCALE * W1_SCALE)
QK_SCALE = 2.0 ** 3
M_SCALE = 2.0 ** 13
MASK_A, MASK_B = 2.0 ** 15, -60000.0

PAIRS = HEADS // 2
BODY_PAIRS = 2
BODIES = BATCH * PAIRS // BODY_PAIRS
QCH = SEQ // CH
QT = SEQ // P
STEPS = sum(2 * i + 2 for i in range(QCH))
UNITS = sum(TPC * (i + 1) for i in range(QCH))
LEAD = 22
S_USES = UNITS + QCH
ST_BANKS, P_SLOTS = 3, 4
PV_LAG, PV_POINT = 3, 1
TURN_DELAY = (2, 7, 4)
OWN_POINTS = (2, 3, 8, 9, 12, 14, 15, 16, 17, 20, 21, 24, 24, 27, 28, 29, 31, 33, 35, 40)
AHEAD_POINTS = (40, 41, 42, 44, 48, 48, 51, 52, 53, 54, 56, 57, 58, 62, 62, 65, 67, 67, 70, 72, 74, 76, 77, 79)


class LayerNormSems:

    def __init__(self, new):
        self.gate = new("gate")
        self.stat = new("stat")
        self.mv = new("mv")
        self.ve = new("ve")
        self.sd = new("sd")
        self.step = new("step")
        self.rstd = new("rstd")
        self.xn = new("xn")


class FfnSems:

    def __init__(self, new):
        self.t_ps = new("t_ps")
        self.xh = new("xh")
        self.xl = new("xl")
        self.l0_ps = new("l0_ps")
        self.l0_hi = new("l0_hi")
        self.l0_lo = new("l0_lo")
        self.l1_ps = new("l1_ps")
        self.l1_hi = new("l1_hi")
        self.l1_lo = new("l1_lo")
        self.l2_ps = new("l2_ps")
        self.res = new("res")


class PhaseASems:

    def __init__(self, new):
        self.x_in = new("x_in")
        self.k0_in = new("k0_in")
        self.k1_in = new("k1_in")
        self.k2_in = new("k2_in")
        self.w_in = new("w_in")
        self.s_in = new("s_in")
        self.bo_in = new("bo_in")
        self.zero = new("zero")
        self.consts = new("consts")
        self.vones = new("vones")
        self.sgn = new("sgn")
        self.sprep = new("sprep")
        self.w0d = new("w0d")
        self.w0 = new("w0")
        self.w1 = new("w1")
        self.w2 = new("w2")
        self.wmax = new("wmax")
        self.wamax = new("wamax")
        self.wchain = new("wchain")
        self.wscale = new("wscale")
        self.wt_ps = new("wt_ps")
        self.wt = new("wt")
        self.t2_ps = new("t2_ps")
        self.x2_t = new("x2_t")
        self.qk_ps = new("qk_ps")
        self.qk_hi = new("qk_hi")
        self.qk_lo = new("qk_lo")
        self.v_ps = new("v_ps")
        self.v_ev = new("v_ev")
        self.qk_st = new("qk_st")
        self.v_st = new("v_st")
        self.gate = new("gate")


class PhaseBSems:

    def __init__(self, new):
        self.rows_zero = new("rows_zero")
        self.rows_const = new("rows_const")
        self.qk_in0 = new("qk_in0")
        self.qk_in1 = new("qk_in1")
        self.v_in0 = new("v_in0")
        self.v_in1 = new("v_in1")
        self.s_ready = new("s_ready")
        self.s_done = new("s_done")
        self.m_neg = new("m_neg")
        self.m_hi = new("m_hi")
        self.m_cols = new("m_cols")
        self.rows_in = new("rows_in")
        self.st_ready = new("st_ready")
        self.exp_done = new("exp_done")
        self.mask_done = new("mask_done")
        self.pv_done = new("pv_done")
        self.ctx_done = new("ctx_done")
        self.ctx_st0 = new("ctx_st0")
        self.ctx_st1 = new("ctx_st1")
        self.gate_pe = new("gate_pe")
        self.gate_pool = new("gate_pool")
        self.bo_add = new("bo_add")


class PhaseCSems:

    def __init__(self, new):
        self.ctx_in = new("ctx_in")
        self.ctx_sum = new("ctx_sum")
        self.wgt_sum = new("wgt_sum")
        self.wgt_inv = new("wgt_inv")
        self.ctx_n = new("ctx_n")
        self.o_ps = new("o_ps")
        self.x2 = new("x2")
        self.out_st = new("out_st")
        self.gate = new("gate")


class LayerNormBuffers:
    def __init__(self, sbuf, sems):
        self.bn = sbuf("bn", [P, TPC, 6], F32)
        self.mv = sbuf("mv", [P, TPC, 2], F32)
        self.ve = sbuf("ve", [P, TPC], F32)
        self.sd = sbuf("sd", [P, TPC], F32)
        self.rs = sbuf("rs", [P, TPC], F32)
        self.nt = sbuf("nt", [P, TPC], F32)
        self.rstd = sbuf("rstd", [P, TPC], F32)
        self.xn = sbuf("xn", [P, TPC, D], F32)
        self.sem = sems


class FfnBuffers:
    def __init__(self, sbuf, psum, sems):
        self.xh = sbuf("xh", [P, DT, CH], F16)
        self.xl = sbuf("xl", [P, DT, CH], F16)
        self.h1h = sbuf("h1h", [P, HT, CH], F16)
        self.h1l = sbuf("h1l", [P, HT, CH], F16)
        self.h2h = sbuf("h2h", [P, HT, CH], F16)
        self.h2l = sbuf("h2l", [P, HT, CH], F16)
        self.mm = psum("mm", [P, 4, CH])
        self.acc = psum("acc", [P, 2, 2 * D])
        self.tr = psum("tr", [P, DT, CH])
        self.sem = sems


def wait(eng, sem, value):
    if not isinstance(value, int) or value > 0:
        eng.wait_ge(sem, value)


def build(nc, x, w_q, w_k, w_v, w_o, b_o, k0, k1, k2, s0, s1, s2, out):
    x_chunks = x.rearrange("b (c t p) d -> (b c) p t d", t=TPC, p=P)
    out_chunks = out.rearrange("b (c t p) d -> (b c) p t d", t=TPC, p=P)
    qk_scr = nc.dram_tensor("qk_scr", (2, 2, BATCH * PAIRS * 2 * DK, SEQ), F16).ap()
    v_scr = nc.dram_tensor("v_scr", (BATCH * PAIRS, SEQ, 64), F32).ap()
    ctx_scr = nc.dram_tensor("ctx_scr", (BATCH * PAIRS, P, SEQ), F32).ap()

    with ExitStack() as top:
        def sbuf(stack, name, shape, dt):
            return stack.enter_context(nc.sbuf_tensor(name, shape, dt))

        def psum(stack, name, shape):
            return stack.enter_context(nc.psum_tensor(name, shape, F32))

        def sem(stack, prefix):
            return lambda name: stack.enter_context(nc.semaphore(prefix + name))

        x_res = sbuf(top, "x_res", [P, NCH * TPC, D], F32)
        w0 = sbuf(top, "w0", [P, DT, HID], F16)
        w1 = sbuf(top, "w1", [P, HT, HID], F16)
        w2 = sbuf(top, "w2", [P, HT, D], F16)
        w_t = sbuf(top, "w_t", [P, 4, DT, D], F32)
        bo_row = sbuf(top, "bo_row", [P, D], F32)
        ident = sbuf(top, "ident", [P, P], F32)
        ident_h = sbuf(top, "ident_h", [P, P], F16)
        ident_mask = sbuf(top, "ident_mask", [P, P], F16)
        mask = sbuf(top, "mask", [P, P], F16)
        ffn_scale = sbuf(top, "ffn_scale", [P, 1], F32)
        qk_scale = sbuf(top, "qk_scale", [P, 2], F32)
        exp_scale = sbuf(top, "exp_scale", [P, 1], F32)

        proj_in = sbuf(top, "proj_in", [P, DT, CH], F32)
        qk_buf = [sbuf(top, f"qk{u}", [P, 4, SEQ], F16) for u in range(2)]
        v_buf = [sbuf(top, f"v{u}", [P, QT, 64], F32) for u in range(2)]
        m_part = [sbuf(top, f"m_part{u}", [P, QT, 2, QCH], F32) for u in range(2)]
        m_neg = sbuf(top, "m_neg", [P, TPC, 2], F32)
        m_col = sbuf(top, "m_col", [P, TPC, 2, 2], F16)
        m_row = sbuf(top, "m_row", [4, CH], F16)
        HEAD_ROWS = (slice(0, 64), slice(64, 128))
        SHIFT_ROWS = (slice(64, 66), slice(0, 2))
        ALL_ROWS = (slice(0, 66), slice(0, 128))

        def load_pair(sp, u, pair):
            for h in range(2):
                for g in range(4):
                    rows = slice(h * 64 + g * DK, h * 64 + (g + 1) * DK)
                    src = bass.ds(pair * 2 * DK + h * DK, DK)
                    sp.dma_start(q_part(u, h, rows, slice(0, SEQ)), qk_scr[g // 2, 0, src, :]).then_inc(qk_in[u], 16)
                    sp.dma_start(k_part(u, h, rows, slice(0, SEQ)), qk_scr[g % 2, 1, src, :]).then_inc(qk_in[u], 16)
            sp.dma_start(v_buf[u][:, :, :], v_scr[bass.ds(pair, 1)].rearrange("o (t p) e -> p (o t) e", p=P)).then_inc(v_in[u], 16)

        def k_part(u, h, rows, cols):
            return qk_buf[u][rows, h, cols]

        def q_part(u, h, rows, cols):
            return qk_buf[u][rows, 2 + h, cols]

        ffn_memory = {}

        def ffn_sbuf(n, shape, dt):
            if n not in ffn_memory:
                ffn_memory[n] = sbuf(top, "ffn_" + n, shape, dt)
            return ffn_memory[n]

        def ffn_psum(n, shape):
            if n not in ffn_memory:
                ffn_memory[n] = psum(top, "ffn_" + n, shape)
            return ffn_memory[n]

        def x_tile(c, t):
            return x_res[:, bass.ds(c * TPC + t, 1), :].rearrange("p o d -> p (o d)")

        def x_tiles(c, t, n):
            return x_res[:, bass.ds(c * TPC + t, n), :].rearrange("p o d -> p (o d)")

        def ln_buffers(name):
            return LayerNormBuffers(lambda n, shape, dt: sbuf(top, f"{name}_{n}", shape, dt), LayerNormSems(sem(top, name + "_")))

        def dve_ln_stats(ln, c):
            for t in range(TPC):
                nc.vector.bn_stats(ln.bn[:, t, :], x_tile(c, t)).then_inc(ln.sem.stat, 1)
            wait(nc.vector, ln.sem.stat, c * TPC + TPC)
            nc.vector.sem_inc(ln.sem.gate, 1)
            for t in range(TPC):
                nc.vector.bn_aggr(ln.mv[:, t, :], ln.bn[:, t, :]).then_inc(ln.sem.mv, 1)
            wait(nc.vector, ln.sem.mv, c * TPC + TPC)
            nc.vector.tensor_scalar(ln.ve[:, :], ln.mv[:, :, 1], EPS, None, ALU.add).then_inc(ln.sem.ve, 1)

        def act_ln_sqrt(ln, c):
            wait(nc.scalar, ln.sem.ve, c + 1)
            nc.scalar.activation(ln.sd[:, :], ln.ve[:, :], ACT.Sqrt).then_inc(ln.sem.sd, 1)

        def dve_ln_finish(ln, c, xn_read):
            wait(nc.vector, ln.sem.sd, c + 1)
            nc.vector.reciprocal(ln.rs[:, :], ln.sd[:, :]).then_inc(ln.sem.step, 1)
            wait(nc.vector, ln.sem.step, c * 4 + 1)
            nc.vector.tensor_tensor(ln.nt[:, :], ln.rs[:, :], ln.rs[:, :], ALU.mult).then_inc(ln.sem.step, 1)
            wait(nc.vector, ln.sem.step, c * 4 + 2)
            nc.vector.tensor_tensor(ln.sd[:, :], ln.nt[:, :], ln.ve[:, :], ALU.mult).then_inc(ln.sem.step, 1)
            wait(nc.vector, ln.sem.step, c * 4 + 3)
            nc.vector.tensor_scalar(ln.nt[:, :], ln.sd[:, :], -0.5, 1.5, ALU.mult, ALU.add).then_inc(ln.sem.step, 1)
            wait(nc.vector, ln.sem.step, c * 4 + 4)
            nc.vector.tensor_tensor(ln.rstd[:, :], ln.rs[:, :], ln.nt[:, :], ALU.mult).then_inc(ln.sem.rstd, 1)
            wait(nc.vector, ln.sem.rstd, c + 1)
            wait(nc.vector, xn_read, c)
            for t in range(TPC):
                ins = nc.vector.tensor_scalar(ln.xn[:, t, :], x_tile(c, t), ln.mv[:, t, 0:1], ln.rstd[:, t:t + 1],
                                              ALU.subtract, ALU.mult)
            ins.then_inc(ln.sem.xn, 1)

        def pe_transpose(ln, ps, done):
            for kt in range(DT):
                for t in range(TPC):
                    ins = nc.tensor.transpose(ps[:, kt, t * P:(t + 1) * P], ln.xn[:, t, kt * P:(kt + 1) * P], ident[:, :])
            ins.then_inc(done, 1)

        def ffn_buffers(name):
            return FfnBuffers(ffn_sbuf, ffn_psum, FfnSems(sem(top, name + "_")))

        def pe_l0(f, c, free):
            wait(nc.tensor, f.sem.xl, c + 1)
            for m in range(HT):
                free(m)
                for kt in range(DT):
                    for part in (f.xh, f.xl):
                        ins = nc.tensor.matmul(f.mm[:, m % 4, :], w0[:, kt, m * P:(m + 1) * P], part[:, kt, :],
                                               start=(kt == 0 and part is f.xh), stop=(kt == DT - 1 and part is f.xl))
                ins.then_inc(f.sem.l0_ps, 1)

        def pe_l1(f, c, ms, free):
            for m in ms:
                free(m)
                for kt in range(HT):
                    if m == 0:
                        wait(nc.tensor, f.sem.l0_lo, c * HT + kt + 1)
                    for part in (f.h1h, f.h1l):
                        ins = nc.tensor.matmul(f.mm[:, m % 4, :], w1[:, kt, m * P:(m + 1) * P], part[:, kt, :],
                                               start=(kt == 0 and part is f.h1h), stop=(kt == HT - 1 and part is f.h1l))
                ins.then_inc(f.sem.l1_ps, 1)

        def pe_l2(f, c, free):
            for t in range(TPC):
                if t % 2 == 0:
                    free(t // 2)
                for kt in range(HT):
                    if t == 0:
                        wait(nc.tensor, f.sem.l1_lo, c * HT + kt + 1)
                    for part in (f.h2h, f.h2l):
                        ins = nc.tensor.matmul(f.acc[:, t // 2, t % 2 * D:(t % 2 + 1) * D], part[:, kt, t * P:(t + 1) * P],
                                               w2[:, kt, :], start=(kt == 0 and part is f.h2h),
                                               stop=(kt == HT - 1 and part is f.h2l))
                if t % 2 == 1:
                    ins.then_inc(f.sem.l2_ps, 1)

        def act_x(f, c):
            wait(nc.scalar, f.sem.t_ps, c + 1)
            wait(nc.scalar, f.sem.l0_ps, c * HT)
            nc.scalar.activation(f.xh[:, :, :], f.tr[:, :, :], ACT.Copy, scale=X_SCALE).then_inc(f.sem.xh, 1)

        def dve_x(f, c):
            wait(nc.vector, f.sem.xh, c + 1)
            for kt in range(DT):
                ins = nc.vector.scalar_tensor_tensor(out=f.xl[:, kt, :], in0=f.tr[:, kt, :], scalar=X_SCALE,
                                                     in1=f.xh[:, kt, :], op0=ALU.mult, op1=ALU.subtract)
            ins.then_inc(f.sem.xl, 1)

        def act_hidden(f, c, ms, layer):
            ps, hi, dst = ((f.sem.l0_ps, f.sem.l0_hi, f.h1h), (f.sem.l1_ps, f.sem.l1_hi, f.h2h))[layer]
            for m in ms:
                if m == 0:
                    if layer == 0:
                        wait(nc.scalar, f.sem.l1_ps, c * HT)
                    else:
                        wait(nc.scalar, f.sem.l2_ps, c * 2)
                wait(nc.scalar, ps, c * HT + m + 1)
                nc.scalar.activation(dst[:, m, :], f.mm[:, m % 4, :], ACT.Relu).then_inc(hi, 1)

        def dve_hidden(f, c, ms, layer):
            hi, lo, src, dst = ((f.sem.l0_hi, f.sem.l0_lo, f.h1h, f.h1l), (f.sem.l1_hi, f.sem.l1_lo, f.h2h, f.h2l))[layer]
            for m in ms:
                wait(nc.vector, hi, c * HT + m + 1)
                nc.vector.scalar_tensor_tensor(out=dst[:, m, :], in0=f.mm[:, m % 4, :], scalar=0.0, in1=src[:, m, :],
                                               op0=ALU.max, op1=ALU.subtract).then_inc(lo, 1)

        def dve_residual(f, c):
            for j in range(2):
                wait(nc.vector, f.sem.l2_ps, c * 2 + j + 1)
                nc.vector.scalar_tensor_tensor(out=x_tiles(c, 2 * j, 2), in0=f.acc[:, j, :], scalar=ffn_scale[:, 0:1],
                                               in1=x_tiles(c, 2 * j, 2), op0=ALU.mult, op1=ALU.add).then_inc(f.sem.res, 1)

        ln1, ln2, ln3 = ln_buffers("ln1"), ln_buffers("ln2"), ln_buffers("ln3")
        fa, fc = ffn_buffers("a"), ffn_buffers("c")
        sa, sb, sc = PhaseASems(sem(top, "a_")), PhaseBSems(sem(top, "b_")), PhaseCSems(sem(top, "c_"))
        qk_in, v_in = (sb.qk_in0, sb.qk_in1), (sb.v_in0, sb.v_in1)
        block = top.enter_context(nc.Block())

        ctx_in = qk_buf[0][:, 0:2, :].bitcast(F32).rearrange("p a (t n) -> p a t n", t=DT)
        wgt_in = qk_buf[0][:, 2:4, :].bitcast(F32).rearrange("p a (t n) -> p a t n", t=DT)

        def load_ctx(sp, b, i):
            for a in range(2):
                for hf in range(DT):
                    src = ctx_scr.rearrange("(b q) (h a e) n -> b a (q h) e n", b=BATCH, h=2, a=2)[
                        bass.ds(b, 1), a, hf * 8:(hf + 1) * 8, :, bass.ds(i * CH, CH)].rearrange("o g e n -> (o g) e n")
                    for dst, e in ((ctx_in, 0), (wgt_in, DK)):
                        sp.dma_start(dst[:, a, hf, :], src[:, e:e + DK, :]).then_inc(sc.ctx_in, 16)

        def pe_out_proj(pe, c, free):
            wait(pe, sc.ctx_n, c + 1)
            for t in range(TPC):
                if t % 2 == 0:
                    free(t // 2)
                for kt in range(DT):
                    ins = nc.tensor.matmul(fc.acc[:, t // 2, t % 2 * D:(t % 2 + 1) * D], proj_in[:, kt, t * P:(t + 1) * P],
                                           w_t[:, 3, kt, :], start=(kt == 0), stop=(kt == DT - 1))
                if t % 2 == 1:
                    ins.then_inc(sc.o_ps, 1)

        with ExitStack() as st:
            k0_u8 = sbuf(st, "k0_u8", [P, 2 * DT, HID], U8)
            k1_u8 = sbuf(st, "k1_u8", [P, HT, HID], U8)
            k2_u8 = sbuf(st, "k2_u8", [P, HT, D], U8)
            w_in = sbuf(st, "w_in", [P, 4, DT, D], F32)
            w_diff = sbuf(st, "w_diff", [P, DT, HID], F16)
            s_in = sbuf(st, "s_in", [P, 3], F32)
            sgn = sbuf(st, "sgn", [P, 3], F32)
            s_abs = sbuf(st, "s_abs", [P, 3], F32)
            s_prod = sbuf(st, "s_prod", [P, 2], F32)
            w0_mul = sbuf(st, "w0_mul", [P, 1], F32)
            w1_mul = sbuf(st, "w1_mul", [P, 1], F32)
            w1_add = sbuf(st, "w1_add", [P, 1], F32)
            w_max = sbuf(st, "w_max", [P, 2], F32)
            w_amax = sbuf(st, "w_amax", [P, 2], F32)
            w_lim = sbuf(st, "w_lim", [P, 2], F32)
            w_pow = sbuf(st, "w_pow", [P, 2], F32)
            w_inv = sbuf(st, "w_inv", [P, 2], F32)
            qk_hi = sbuf(st, "qk_hi", [P, 2 * DT, CH], F16)
            qk_lo = sbuf(st, "qk_lo", [P, 2 * DT, CH], F16)
            v_pad = sbuf(st, "v_pad", [P, TPC, HEADS, 32], F32)
            f = fa
            se = sa

            def pe_t1(c, first=False):
                wait(nc.tensor, ln1.sem.xn, c + 1)
                if first:
                    wait(nc.tensor, f.sem.xl, c)
                else:
                    wait(nc.tensor, se.x2_t, c - 1)
                pe_transpose(ln1, f.tr, f.sem.t_ps)

            def pe_t2(c, last=False):
                wait(nc.tensor, ln2.sem.xn, c + 1)
                if last:
                    wait(nc.tensor, se.x2_t, c)
                else:
                    wait(nc.tensor, f.sem.xl, c + 2)
                pe_transpose(ln2, f.tr, se.t2_ps)

            def pe_qkv(c, last=False):
                wait(nc.tensor, se.x2_t, c + 1)
                for j in range(2 * DT):
                    if not last:
                        wait(nc.tensor, f.sem.l1_lo, (c + 1) * HT + j + 1)
                    for kt in range(DT):
                        ins = nc.tensor.matmul(f.mm[:, j, :], w_t[:, j // DT, kt, j % DT * P:(j % DT + 1) * P],
                                               proj_in[:, kt, :], start=(kt == 0), stop=(kt == DT - 1))
                    ins.then_inc(se.qk_ps, 1)
                for t in range(TPC):
                    if t % 2 == 0:
                        wait(nc.tensor, f.sem.res, c * 2 + t // 2 + 1)
                    for kt in range(DT):
                        ins = nc.tensor.matmul(f.acc[:, t // 2, t % 2 * D:(t % 2 + 1) * D], proj_in[:, kt, t * P:(t + 1) * P],
                                               w_t[:, 2, kt, :], start=(kt == 0), stop=(kt == DT - 1))
                    if t % 2 == 1:
                        ins.then_inc(se.v_ps, 1)

            def act_x2(c):
                wait(nc.scalar, se.t2_ps, c + 1)
                wait(nc.scalar, se.v_ps, c * 2)
                nc.scalar.activation(proj_in[:, :, :], f.tr[:, :, :], ACT.Copy).then_inc(se.x2_t, 1)

            def act_qkv(c):
                for j in range(2 * DT):
                    if j == 0:
                        wait(nc.scalar, se.qk_st, c * 128)
                    wait(nc.scalar, se.qk_ps, c * 4 + j + 1)
                    nc.scalar.activation(qk_hi[:, j, :], f.mm[:, j, :], ACT.Copy,
                                         scale=qk_scale[:, j // DT:j // DT + 1]).then_inc(se.qk_hi, 1)
                for j in range(2):
                    if j == 0:
                        wait(nc.scalar, se.v_st, c * 64)
                    wait(nc.scalar, se.v_ps, c * 2 + j + 1)
                    nc.scalar.activation(v_pad[:, 2 * j:2 * j + 2, :, 0:DK].rearrange("p t h d -> p (t h) d"),
                                         f.acc[:, j, :].rearrange("p (g d) -> p g d", d=DK),
                                         ACT.Copy).then_inc(se.v_ev, 1)

            def dve_qk(c):
                for j in range(2 * DT):
                    wait(nc.vector, se.qk_hi, c * 4 + j + 1)
                    nc.vector.scalar_tensor_tensor(out=qk_lo[:, j, :], in0=f.mm[:, j, :],
                                                   scalar=qk_scale[:, j // DT:j // DT + 1], in1=qk_hi[:, j, :],
                                                   op0=ALU.mult, op1=ALU.subtract).then_inc(se.qk_lo, 1)

            @block.sync
            def _(sp):
                sp.dma_start(x_res[:, 0:TPC, :], x_chunks[0]).then_inc(se.x_in, 16)
                sp.dma_start(k0_u8[:, :, :], k0.rearrange("(t p) f -> p t f", p=P)).then_inc(se.k0_in, 16)
                for n, s in enumerate((s0, s1, s2)):
                    sp.dma_start(s_in[:, n:n + 1], s.rearrange("(a b) -> a b", a=1).to_broadcast([P, 1])).then_inc(se.s_in, 16)
                sp.dma_start(k1_u8[:, :, :], k1.rearrange("(t p) f -> p t f", p=P)).then_inc(se.k1_in, 16)
                for n, w in enumerate((w_q, w_k, w_v, w_o)):
                    sp.dma_start(w_in[:, n, :, :], w.rearrange("(t p) d -> p t d", p=P)).then_inc(se.w_in, 16)
                sp.dma_start(k2_u8[:, :, :], k2.rearrange("(t p) f -> p t f", p=P)).then_inc(se.k2_in, 16)
                sp.dma_start(bo_row[:, :], b_o.rearrange("(a d) -> a d", a=1).to_broadcast([P, D])).then_inc(se.bo_in, 16)
                with sp.Fori(1, NCH) as c:
                    wait(sp, se.x_in, c * 16)
                    sp.dma_start(x_res[:, bass.ds(c * TPC, TPC), :],
                                 x_chunks[bass.ds(c, 1)].rearrange("o p t d -> (o p) t d")).then_inc(se.x_in, 16)

                def store(b, i):
                    for n, part in enumerate((qk_hi, qk_lo)):
                        if n == 0:
                            wait(sp, se.qk_lo, b * (QCH * 4) + i * 4 + 4)
                        for j in range(2 * DT):
                            sp.dma_start(qk_scr[n, j // DT, b * D + j % DT * P:b * D + (j % DT + 1) * P, bass.ds(i * CH, CH)],
                                         part[:, j, :]).then_inc(se.qk_st, 16)
                    wait(sp, se.v_ev, b * (QCH * 2) + i * 2 + 2)
                    for t in range(TPC):
                        sp.dma_start(v_scr[b * PAIRS:(b + 1) * PAIRS, bass.ds(i * CH + t * P, P), :].rearrange("g p e -> p g e"),
                                     v_pad[:, t, :, :].rearrange("p (g h) e -> p g (h e)", h=2)).then_inc(se.v_st, 16)

                with sp.Fori(0, QCH) as i:
                    store(0, i)
                sp.wait_ge(se.qk_st, QCH * 128)
                sp.wait_ge(se.v_st, QCH * 64)
                sp.wait_ge(sb.rows_const, 4)
                load_pair(sp, 0, 0)
                with sp.Fori(0, QCH) as i:
                    store(1, i)

            @block.gpsimd
            def _(pool):
                nc.gpsimd.memset(ident[:, :], 0.0).then_inc(se.zero, 1)
                nc.gpsimd.memset(mask[:, :], 0.0).then_inc(se.zero, 1)
                nc.gpsimd.memset(v_pad[:, :, :, DK:32], 1.0).then_inc(se.vones, 1)
                pool.wait_ge(se.zero, 2)
                nc.gpsimd.affine_select(out=ident[:, :], in_=ident[:, :], compare_op=ALU.not_equal, fill=1.0, base=0,
                                        pattern=[[-1, P]], channel_multiplier=1).then_inc(se.consts, 1)
                nc.gpsimd.affine_select(out=mask[:, :], in_=mask[:, :], compare_op=ALU.is_ge, fill=MASK_B, base=0,
                                        pattern=[[-1, P]], channel_multiplier=1).then_inc(se.consts, 1)
                pool.wait_ge(se.consts, 2)
                nc.gpsimd.tensor_copy(ident_h[:, :], ident[:, :]).then_inc(se.consts, 1)
                nc.gpsimd.tensor_scalar(ident_mask[:, :], ident[:, :], MASK_A, 0.0, ALU.mult, ALU.add).then_inc(se.consts, 1)
                pool.wait_ge(se.k1_in, 16)
                pool.wait_ge(se.sprep, 3)
                nc.gpsimd.tensor_scalar(w1[:, HT // 2:, :], k1_u8[:, HT // 2:, :], w1_mul[:, 0:1], w1_add[:, 0:1],
                                        ALU.mult, ALU.add).then_inc(se.w1, 1)
                pool.wait_ge(se.wmax, 2)
                nc.gpsimd.partition_all_reduce(w_amax[:, :], w_max[:, :], P, RMAX).then_inc(se.wamax, 1)
                pool.wait_ge(se.wamax, 1)
                for u in range(2):
                    nc.gpsimd.memset(k_part(u, 0, SHIFT_ROWS[0], slice(0, SEQ)), M_SCALE).then_inc(sb.rows_const, 1)
                    nc.gpsimd.memset(k_part(u, 1, slice(0, 64), slice(0, SEQ)), 0.0).then_inc(sb.rows_zero, 1)
                    nc.gpsimd.memset(q_part(u, 1, slice(0, 64), slice(0, SEQ)), 0.0).then_inc(sb.rows_zero, 1)
                pool.wait_ge(sb.rows_zero, 4)
                for u in range(2):
                    nc.gpsimd.memset(k_part(u, 1, SHIFT_ROWS[1], slice(0, SEQ)), M_SCALE).then_inc(sb.rows_const, 1)
                pool.wait_ge(se.bo_in, 16)
                with pool.Fori(0, NCH) as c:
                    pool.wait_ge(ln2.sem.xn, c + 1)
                    pool.sem_inc(sb.gate_pool, 1)
                    for t in range(TPC):
                        nc.gpsimd.tensor_tensor(x_tile(c, t), x_tile(c, t), bo_row[:, :], ALU.add).then_inc(sb.bo_add, 1)

            @block.vector
            def _(dve):
                dve.wait_ge(se.x_in, 16)
                dve_ln_stats(ln1, 0)
                dve.wait_ge(se.s_in, 48)
                nc.vector.tensor_scalar(sgn[:, :], s_in[:, :], 0.0, 2.0, ALU.is_ge, ALU.mult).then_inc(se.sgn, 1)
                dve.wait_ge(se.sgn, 1)
                nc.vector.tensor_scalar(s_abs[:, :], sgn[:, :], -1.0, None, ALU.add).then_inc(se.sgn, 1)
                dve.wait_ge(se.sgn, 2)
                nc.vector.tensor_scalar(w0_mul[:, :], s_abs[:, 0:1], 2.0 * W0_SCALE, None, ALU.mult).then_inc(se.sprep, 1)
                nc.vector.tensor_scalar(w1_mul[:, :], s_abs[:, 1:2], 2.0 * W1_SCALE, None, ALU.mult).then_inc(se.sprep, 1)
                nc.vector.tensor_scalar(w1_add[:, :], s_abs[:, 1:2], -W1_SCALE, None, ALU.mult).then_inc(se.sprep, 1)
                nc.vector.tensor_tensor(s_prod[:, :], s_abs[:, 0:2], s_in[:, 0:2], ALU.mult).then_inc(se.sgn, 1)
                dve.wait_ge(se.k0_in, 16)
                nc.vector.tensor_tensor(w_diff[:, :, :], k0_u8[:, 0:DT, :], k0_u8[:, DT:, :], ALU.subtract).then_inc(se.w0d, 1)
                dve_ln_finish(ln1, 0, f.sem.t_ps)
                dve.wait_ge(se.w0d, 1)
                dve.wait_ge(se.sprep, 1)
                nc.vector.tensor_scalar(w0[:, :, :], w_diff[:, :, :], w0_mul[:, 0:1], None, ALU.mult).then_inc(se.w0, 1)
                dve_x(f, 0)
                dve.wait_ge(se.k1_in, 16)
                dve.wait_ge(se.sprep, 3)
                nc.vector.tensor_scalar(w1[:, 0:HT // 2, :], k1_u8[:, 0:HT // 2, :], w1_mul[:, 0:1], w1_add[:, 0:1],
                                        ALU.mult, ALU.add).then_inc(se.w1, 1)
                dve_hidden(f, 0, range(HT), 0)
                dve.wait_ge(se.sgn, 3)
                nc.vector.tensor_tensor(s_prod[:, 0:1], s_prod[:, 0:1], s_prod[:, 1:2], ALU.mult).then_inc(se.sgn, 1)
                dve.wait_ge(se.sgn, 4)
                nc.vector.tensor_scalar(ffn_scale[:, :], s_prod[:, 0:1], s_in[:, 2:3], 2.0 * FFN_UNSCALE,
                                        ALU.mult, ALU.mult).then_inc(se.sgn, 1)
                dve.wait_ge(se.k2_in, 16)
                nc.vector.tensor_scalar(w2[:, :, :], k2_u8[:, :, :], 2.0, -1.0, ALU.mult, ALU.add).then_inc(se.w2, 1)
                dve.wait_ge(se.w_in, 64)
                for n in range(2):
                    nc.vector.tensor_reduce(w_max[:, n:n + 1], w_in[:, n, :, :], AX.XY, ALU.max,
                                            apply_absolute_value=True).then_inc(se.wmax, 1)
                dve.wait_ge(se.x_in, 32)
                dve_ln_stats(ln1, 1)
                dve_ln_finish(ln1, 1, f.sem.t_ps)
                dve.wait_ge(se.wamax, 1)
                nc.vector.tensor_scalar(w_lim[:, :], w_amax[:, :], 2.0 ** -60, None, ALU.max).then_inc(se.wchain, 1)
                dve.wait_ge(se.wchain, 1)
                nc.vector.tensor_scalar(w_pow[:, :].bitcast(U32), w_lim[:, :].bitcast(U32), 0x7F800000, None,
                                        ALU.bitwise_and).then_inc(se.wchain, 1)
                dve.wait_ge(se.wchain, 2)
                nc.vector.reciprocal(w_inv[:, :], w_pow[:, :]).then_inc(se.wchain, 1)
                nc.vector.tensor_scalar(exp_scale[:, :], w_pow[:, 0:1], w_pow[:, 1:2],
                                        DK ** -0.5 / QK_SCALE ** 2, ALU.mult, ALU.mult).then_inc(se.wscale, 1)
                dve.wait_ge(se.wchain, 3)
                nc.vector.tensor_scalar(qk_scale[:, :], w_inv[:, :], QK_SCALE, None, ALU.mult).then_inc(se.wscale, 1)
                dve.wait_ge(se.sgn, 5)

                def chunk(c, first=False, last=False):
                    dve_hidden(f, c, range(0, 4), 1)
                    if not first:
                        dve_qk(c - 1)
                    dve_hidden(f, c, range(4, 6), 1)
                    if not last:
                        dve_x(f, c + 1)
                    dve_hidden(f, c, range(6, HT), 1)
                    dve_residual(f, c)
                    if not last:
                        dve_hidden(f, c + 1, range(HT), 0)
                    wait(dve, f.sem.res, c * 2 + 2)
                    dve.sem_inc(se.gate, 1)
                    dve_ln_stats(ln2, c)

                def next_ln(c):
                    wait(dve, se.x_in, (c + 3) * 16)
                    dve.sem_inc(se.gate, 1)
                    dve_ln_stats(ln1, c + 2)
                    dve_ln_finish(ln2, c, se.t2_ps)
                    dve_ln_finish(ln1, c + 2, f.sem.t_ps)

                chunk(0, first=True)
                next_ln(0)
                with dve.Fori(1, NCH - 2) as c:
                    chunk(c)
                    next_ln(c)
                chunk(NCH - 2)
                dve_ln_finish(ln2, NCH - 2, se.t2_ps)
                chunk(NCH - 1, last=True)
                dve_ln_finish(ln2, NCH - 1, se.t2_ps)
                dve_qk(NCH - 1)

            @block.scalar
            def _(act):
                act_ln_sqrt(ln1, 0)
                act_x(f, 0)
                for n in range(4):
                    act.wait_ge(se.wt_ps, n + 1)
                    nc.scalar.activation(w_t[:, n, :, :], f.mm[:, n, :].rearrange("p (t d) -> p t d", t=DT),
                                         ACT.Copy).then_inc(se.wt, 1)
                act_hidden(f, 0, range(HT), 0)
                act_ln_sqrt(ln1, 1)
                act.wait_ge(se.wscale, 2)
                act.wait_ge(se.vones, 1)

                def chunk(c, first=False, last=False):
                    act_hidden(f, c, range(0, 3), 1)
                    if not first:
                        act_x2(c - 1)
                    act_hidden(f, c, range(3, 4), 1)
                    if not first:
                        act_qkv(c - 1)
                    act_hidden(f, c, range(4, 6), 1)
                    if not last:
                        act_x(f, c + 1)
                    act_hidden(f, c, range(6, HT), 1)
                    if not last:
                        act_hidden(f, c + 1, range(HT), 0)
                    act_ln_sqrt(ln2, c)

                chunk(0, first=True)
                act_ln_sqrt(ln1, 2)
                chunk(1)
                act_ln_sqrt(ln1, 3)
                with act.Fori(2, NCH - 2) as c:
                    chunk(c)
                    act_ln_sqrt(ln1, c + 2)
                chunk(NCH - 2)
                chunk(NCH - 1, last=True)
                act_x2(NCH - 1)
                act_qkv(NCH - 1)

            @block.tensor
            def _(pe):
                pe.wait_ge(se.consts, 2)
                pe_t1(0, first=True)
                pe.wait_ge(se.w_in, 64)
                for n in range(4):
                    for jt in range(DT):
                        for it in range(DT):
                            ins = nc.tensor.transpose(f.mm[:, n, it * D + jt * P:it * D + (jt + 1) * P],
                                                      w_in[:, n, jt, it * P:(it + 1) * P], ident[:, :])
                    ins.then_inc(se.wt_ps, 1)
                pe.wait_ge(se.w0, 1)

                def l0_free(c):
                    def free(m):
                        if m < 4 and isinstance(c, int) and c == 0:
                            wait(pe, se.wt, m + 1)
                        elif m < 4:
                            wait(pe, f.sem.l1_lo, (c - 1) * HT + 5 + m)
                        else:
                            wait(pe, f.sem.l0_lo, c * HT + m - 3)
                    return free

                def l1_free(c, first):
                    def free(m):
                        if m == 0:
                            wait(pe, f.sem.l0_lo, c * HT + 5)
                        elif m >= 4 and first:
                            wait(pe, f.sem.l1_lo, c * HT + m - 3)
                        elif m >= 4:
                            wait(pe, se.qk_lo, (c - 1) * 4 + m - 3)
                    return free

                def l2_free(c, first):
                    def free(j):
                        if not first:
                            wait(pe, se.v_ev, (c - 1) * 2 + j + 1)
                    return free

                def chunk(c, first=False, last=False):
                    pe_l1(f, c, range(0, 3), l1_free(c, first))
                    if not first:
                        pe_t2(c - 1)
                    pe_l1(f, c, range(3, 4), l1_free(c, first))
                    if not first:
                        pe_qkv(c - 1)
                    pe_l1(f, c, range(4, 6), l1_free(c, first))
                    if not last:
                        pe_t1(c + 1, first=first)
                    pe_l1(f, c, range(6, HT), l1_free(c, first))
                    pe_l2(f, c, l2_free(c, first))
                    if not last:
                        pe_l0(f, c + 1, l0_free(c + 1))

                pe_l0(f, 0, l0_free(0))
                pe.wait_ge(se.w1, 2)
                pe.wait_ge(se.w2, 1)
                chunk(0, first=True)
                with pe.Fori(1, NCH - 1) as c:
                    chunk(c)
                chunk(NCH - 1, last=True)
                pe_t2(NCH - 1, last=True)
                pe_qkv(NCH - 1, last=True)

        with ExitStack() as st:
            probs = sbuf(st, "probs", [P, P_SLOTS, 4, CH], F32)
            ctx_out = sbuf(st, "ctx_out", [P, 2, CH], F32)
            s_ps = (fa.tr, fa.acc)
            st_ps = [fa.mm[:, n, :] for n in range(ST_BANKS)]
            ctx_ps = fa.mm[:, 3, :]
            se = sb
            ctx_st = (se.ctx_st0, se.ctx_st1)

            units = [("unit", t, r) for i in range(QCH) for t in range(TPC * i, TPC * i + TPC) for r in range(i + 1)]
            last_unit = {i: max(n for n, x in enumerate(units) if x[1] // TPC == i) for i in range(QCH)}

            def with_turns(lo, hi):
                seq = []
                for n in range(lo, hi):
                    seq.append(units[n])
                    seq += [("turn", i) for i in range(QCH - 1) if last_unit[i] + TURN_DELAY[i] == n]
                return seq

            AHEAD = with_turns(0, LEAD)
            OWN = with_turns(LEAD, UNITS) + [("turn", QCH - 1)]
            assert len(AHEAD) == len(AHEAD_POINTS) and len(OWN) == len(OWN_POINTS)
            assert len(AHEAD) + len(OWN) == S_USES and len(AHEAD) % 2 == 0 and S_USES % 2 == 0

            chunk_of = [i for i in range(QCH) for _ in range(2 * i + 2)]
            first_step = [chunk_of.index(i) for i in range(QCH)]

            def step_slots(s):
                i = chunk_of[s]
                out = []
                for par in range(2):
                    kb = 2 * (s - first_step[i]) + par
                    c0 = max(0, (kb - TPC * i) * P)
                    if kb == 1 and i == 0:
                        c0 = 0
                    for h in range(2):
                        out.append((kb, h, c0))
                return out

            def schedule(u, last):
                plan = [[] for _ in range(4 * STEPS)]
                work = [(u, x) for x in OWN] + [(1 - u, x) for x in AHEAD]
                for use, ((buf, x), point) in enumerate(zip(work, OWN_POINTS + AHEAD_POINTS)):
                    if buf == u or not last:
                        plan[point].append((buf, x, use))
                return plan

            def diagonal(s):
                return chunk_of[s] * TPC <= step_slots(s)[0][0]

            body_steps = [(u, s) for u in range(BODY_PAIRS) for s in range(STEPS)]
            LOAD_STEP = AHEAD_POINTS[0] // 4
            OUT_PROJ_STEP = STEPS - 7
            EXPS, NSTEP = 4 * len(body_steps), len(body_steps)

            @block.sync
            def _(sp):
                def rows(u, i, turn, use):
                    wait(sp, se.s_done, use + 1)
                    for h in range(2):
                        sp.dma_start(q_part(u, h, SHIFT_ROWS[h], slice(i * CH, (i + 1) * CH)),
                                     m_row[2 * h:2 * h + 2, :]).then_inc(se.rows_in, 16)

                def store(pair, n, i):
                    wait(sp, se.ctx_done, n + 1)
                    sp.dma_start(ctx_scr[bass.ds(pair, 1), :, i * CH:(i + 1) * CH].rearrange("o p n -> (o p) n"),
                                 ctx_out[:, i % 2, :]).then_inc(ctx_st[i % 2], 16)

                def body(it, last):
                    for u in range(BODY_PAIRS):
                        pair = it * BODY_PAIRS + u
                        base = pair * S_USES + len(AHEAD)
                        turns = [(b, x[1], use) for step in schedule(u, last and u == 1) for b, x, use in step if x[0] == "turn"]
                        order = [turns[0], "load", 0, 1, turns[1]] + turns[2:3] + [2] + turns[3:4] + [3]
                        for x in order:
                            if x == "load":
                                wait(sp, se.pv_done, pair * STEPS)
                                if last and u == 1:
                                    load_ctx(sp, 0, 0)
                                else:
                                    load_pair(sp, 1 - u, pair + 1)
                                continue
                            if last and u == 1 and x == QCH - 2:
                                wait(sp, sc.ctx_n, 1)
                                load_ctx(sp, 0, 1)
                            if isinstance(x, int):
                                store(pair, pair * QCH + x, x)
                            else:
                                rows(x[0], x[1], None, base + x[2])

                sp.wait_ge(sa.qk_st, NCH * 128)
                sp.wait_ge(sa.v_st, NCH * 64)
                for n, x in enumerate(AHEAD):
                    if x[0] == "turn":
                        rows(0, x[1], None, n)
                body(0, False)
                with sp.Fori(1, BODIES - 1) as it:
                    body(it, False)
                body(BODIES - 1, True)
                for sem in ctx_st:
                    sp.wait_ge(sem, 8 * BATCH * PAIRS * QCH)

            @block.gpsimd
            def _(pool):
                def body(it):
                    for g, (u, s) in enumerate(body_steps):
                        if not diagonal(s):
                            continue
                        i = chunk_of[s]
                        for par in range(2):
                            kb, _, c0 = step_slots(s)[2 * par]
                            w = (kb - TPC * i + 1) * P - c0
                            pool.wait_ge(se.exp_done, it * EXPS + 4 * g + 2 * par + 2)
                            pool.sem_inc(se.gate_pool, 1)
                            view = probs[:, g % P_SLOTS, 2 * par:2 * par + 2, c0:c0 + w]
                            nc.gpsimd.affine_select(out=view, in_=view, compare_op=ALU.is_ge, fill=0.0,
                                                    base=c0 - (kb - TPC * i) * P, pattern=[[0, 2], [1, w]],
                                                    channel_multiplier=-1).then_inc(se.mask_done, 1)

                with pool.Fori(0, BODIES - 1) as it:
                    body(it)
                body(BODIES - 1)

            @block.vector
            def _(dve):
                def item(u, x, use, turns_before):
                    wait(dve, se.s_ready, use + 1)
                    slot = use_slot(use_static[0])
                    if x[0] == "unit":
                        _, t, r = x
                        w = CH if r < t // TPC else (t % TPC + 1) * P
                        nc.vector.tensor_reduce(m_part[u][:, t, :, r], s_ps[slot][:, :, 0:w], AX.X, ALU.max).then_inc(se.s_done, 1)
                        i = t // TPC
                        if units.index(x) == last_unit[i]:
                            n = turns_before + 1
                            wait(dve, se.s_done, use + 1)
                            nc.vector.tensor_reduce(m_neg[:, :, :], m_part[u][:, i * TPC:(i + 1) * TPC, :, 0:i + 1], AX.X,
                                                    ALU.max, negate=True).then_inc(se.m_neg, 1)
                            wait(dve, se.m_neg, n)
                            nc.vector.tensor_scalar(m_col[:, :, :, 0], m_neg[:, :, :], 1.0 / M_SCALE, None,
                                                    ALU.mult).then_inc(se.m_hi, 1)
                            wait(dve, se.m_hi, n)
                            nc.vector.scalar_tensor_tensor(out=m_col[:, :, :, 1], in0=m_neg[:, :, :], scalar=1.0 / M_SCALE,
                                                           in1=m_col[:, :, :, 0], op0=ALU.mult,
                                                           op1=ALU.subtract).then_inc(se.m_cols, 1)
                    else:
                        wait(dve, se.rows_in, turns_before * 32)
                        nc.vector.tensor_copy(m_row[:, :], s_ps[slot][0:4, 0, :]).then_inc(se.s_done, 1)

                use_static = [0]

                def use_slot(n):
                    return n % 2

                def chunk_number(pair, i):
                    return pair * QCH + i

                for n, x in enumerate(AHEAD):
                    use_static[0] = n
                    i = x[1] if x[0] == "turn" else x[1] // TPC
                    item(0, x, n, chunk_number(0, i))

                def body(it, last):
                    for u in range(BODY_PAIRS):
                        pair = it * BODY_PAIRS + u
                        for step in schedule(u, last and u == 1):
                            for buf, x, use in step:
                                use_static[0] = use
                                i = x[1] if x[0] == "turn" else x[1] // TPC
                                owner = pair if buf == u else pair + 1
                                item(buf, x, pair * S_USES + len(AHEAD) + use, chunk_number(owner, i))

                with dve.Fori(0, BODIES - 1) as it:
                    body(it, False)
                body(BODIES - 1, True)

            @block.scalar
            def _(act):
                ends = [g + PV_LAG for g, (u, s) in enumerate(body_steps) if s + 1 == STEPS or chunk_of[s + 1] != chunk_of[s]]

                act.wait_ge(sa.qk_st, NCH * 128)
                act.wait_ge(sa.v_st, NCH * 64)

                def body(it, last=False):
                    def evacuate(n):
                        wait(act, se.pv_done, it * NSTEP + ends[n] - PV_LAG + 1)
                        wait(act, ctx_st[n % 2], it * (BODY_PAIRS * QCH * 8) + n // 2 * 16)
                        nc.scalar.activation(ctx_out[:, n % 2, :], ctx_ps[:, :], ACT.Copy).then_inc(se.ctx_done, 1)

                    for g, (u, s) in enumerate(body_steps):
                        for j, (kb, h, c0) in enumerate(step_slots(s)):
                            k = 4 * g + j
                            if j == 0:
                                wait(act, se.pv_done, it * NSTEP + max(0, g - P_SLOTS + 1))
                            wait(act, se.st_ready, it * EXPS + k + 1)
                            nc.scalar.activation(probs[:, g % P_SLOTS, j, c0:CH], st_ps[k % ST_BANKS][:, c0:CH], ACT.Exp,
                                                 scale=exp_scale[:, 0:1]).then_inc(se.exp_done, 1)
                            if j == PV_POINT and g in ends:
                                evacuate(ends.index(g))
                    if last:
                        act_ln_sqrt(ln3, 0)
                    for n, g in enumerate(ends):
                        if g >= NSTEP:
                            evacuate(n)

                body(0)
                with act.Fori(1, BODIES - 1) as it:
                    body(it)
                body(BODIES - 1, last=True)

            @block.tensor
            def _(pe):
                def item(u, x, use, slot, cols):
                    wait(pe, se.s_done, use - 1)
                    if x[0] == "unit":
                        _, t, r = x
                        i = t // TPC
                        w = CH if r < i else (t % TPC + 1) * P
                        pe.sem_inc(se.gate_pe, 1)
                        for h in range(2):
                            ins = nc.tensor.matmul(s_ps[slot][:, h, 0:w], q_part(u, h, HEAD_ROWS[h], slice(t * P, (t + 1) * P)),
                                                   k_part(u, h, HEAD_ROWS[h], slice(r * CH, r * CH + w)), start=True, stop=(r < i))
                        if r == i:
                            for h in range(2):
                                ins = nc.tensor.matmul(s_ps[slot][:, h, w - P:w], ident_mask[:, :], mask[:, :],
                                                       start=False, stop=True)
                    else:
                        wait(pe, se.m_cols, cols)
                        for t in range(TPC):
                            ins = nc.tensor.matmul(s_ps[slot][0:4, 0, t * P:(t + 1) * P],
                                                   m_col[:, t, :, :].rearrange("p h a -> p (h a)"), ident_h[:, :],
                                                   start=True, stop=True)
                    ins.then_inc(se.s_ready, 1)

                def load_wait(u, it):
                    pe.wait_ge(qk_in[u], (it + 1) * 256)
                    pe.sem_inc(se.gate_pe, 1)

                load_wait(0, 0)
                for n, x in enumerate(AHEAD):
                    if n == 1:
                        pe.wait_ge(sa.v_ev, NCH * 2)
                    item(0, x, n, n % 2, x[1] + 1)
                pe.wait_ge(sa.qk_lo, NCH * 4)

                def body(it, last):
                    def scores(g, j):
                        u, s = body_steps[g]
                        i = chunk_of[s]
                        kb, h, c0 = step_slots(s)[j]
                        k = 4 * g + j
                        if j == 0 and s == first_step[i]:
                            wait(pe, se.rows_in, (it * BODY_PAIRS + u) * (QCH * 32) + (i + 1) * 32)
                        wait(pe, se.exp_done, it * EXPS + (max(0, k - ST_BANKS + 1)))
                        rows = ALL_ROWS[h]
                        nc.tensor.matmul(st_ps[k % ST_BANKS][:, c0:CH], k_part(u, h, rows, slice(kb * P, (kb + 1) * P)),
                                         q_part(u, h, rows, slice(i * CH + c0, (i + 1) * CH)), start=True, stop=True).then_inc(se.st_ready, 1)

                    def products(g):
                        u, s = body_steps[g]
                        i = chunk_of[s]
                        first = s == first_step[i]
                        final = s + 1 == STEPS or chunk_of[s + 1] != i
                        if s == 0:
                            wait(pe, v_in[u], (it + 1) * 16)
                        if first:
                            wait(pe, se.ctx_done, (it * BODY_PAIRS + u) * QCH + i)
                        if diagonal(s):
                            wait(pe, se.mask_done, (it * BODY_PAIRS + u) * (QCH * TPC) + i * TPC + 2 * (s - first_step[i] - 2 * i) + 2)
                        wait(pe, se.exp_done, it * EXPS + 4 * g + 4)
                        for j, (kb, h, c0) in enumerate(step_slots(s)):
                            row = 32 * (2 * h + kb % 2)
                            ins = nc.tensor.matmul(ctx_ps[row:row + 32, c0:CH], v_buf[u][:, kb, h * 32:(h + 1) * 32],
                                                   probs[:, g % P_SLOTS, j, c0:CH], start=first, stop=final,
                                                   tile_position=(0, row))
                        ins.then_inc(se.pv_done, 1)

                    plans = [schedule(u, last and u == 1) for u in range(BODY_PAIRS)]
                    for g, (u, s) in enumerate(body_steps):
                        pair = it * BODY_PAIRS + u
                        if s == LOAD_STEP and not (last and u == 1):
                            load_wait(1 - u, it + u)
                        for j in range(4):
                            scores(g, j)
                            if j == PV_POINT and g >= PV_LAG:
                                products(g - PV_LAG)
                            for b, x, use in plans[u][4 * s + j]:
                                owner = pair if b == u else pair + 1
                                cols = owner * QCH + x[1] + 1 if x[0] == "turn" else None
                                item(b, x, pair * S_USES + len(AHEAD) + use, use % 2, cols)
                        if last and u == 1 and s == OUT_PROJ_STEP:
                            wait(pe, se.s_done, BATCH * PAIRS * S_USES)
                            pe_out_proj(pe, 0, lambda j: None)
                    for g in range(NSTEP - PV_LAG, NSTEP):
                        products(g)

                body(0, False)
                with pe.Fori(1, BODIES - 1) as it:
                    body(it, False)
                body(BODIES - 1, True)

        with ExitStack() as st:
            f = fc
            se = sc

            def load_done(c):
                return c * 128 + 128

            @block.sync
            def _(sp):
                with sp.Fori(2, NCH) as c:
                    wait(sp, se.ctx_n, c)
                    load_ctx(sp, c // QCH, c % QCH)
                with sp.Fori(0, NCH) as c:
                    wait(sp, f.sem.res, c * 2 + 2)
                    sp.dma_start(out_chunks[bass.ds(c, 1)].rearrange("o p t d -> (o p) t d"),
                                 x_res[:, bass.ds(c * TPC, TPC), :]).then_inc(se.out_st, 16)
                sp.wait_ge(se.out_st, NCH * 16)

            @block.vector
            def _(dve):
                def normalize(c):
                    wait(dve, se.ctx_in, load_done(c))
                    dve.sem_inc(se.gate, 1)
                    nc.vector.tensor_tensor(wgt_in[:, 0, :, :], wgt_in[:, 0, :, :], wgt_in[:, 1, :, :], ALU.add).then_inc(se.wgt_sum, 1)
                    nc.vector.tensor_tensor(ctx_in[:, 0, :, :], ctx_in[:, 0, :, :], ctx_in[:, 1, :, :], ALU.add).then_inc(se.ctx_sum, 1)
                    wait(dve, se.wgt_sum, c + 1)
                    nc.vector.reciprocal(wgt_in[:, 0, :, :], wgt_in[:, 0, :, :]).then_inc(se.wgt_inv, 1)
                    wait(dve, se.wgt_inv, c + 1)
                    wait(dve, se.ctx_sum, c + 1)
                    wait(dve, se.o_ps, c * 2)
                    nc.vector.tensor_tensor(proj_in[:, :, :], ctx_in[:, 0, :, :], wgt_in[:, 0, :, :], ALU.mult).then_inc(se.ctx_n, 1)

                def add_attention(c):
                    for j in range(2):
                        wait(dve, se.o_ps, c * 2 + j + 1)
                        nc.vector.tensor_tensor(x_tiles(c, 2 * j, 2), f.acc[:, j, :], x_tiles(c, 2 * j, 2), ALU.add).then_inc(se.x2, 1)
                    wait(dve, se.x2, c * 2 + 2)
                    dve.sem_inc(se.gate, 1)
                    dve_ln_stats(ln3, c)
                    if isinstance(c, int) and c == 0:
                        normalize(1)
                    dve_ln_finish(ln3, c, f.sem.t_ps)

                normalize(0)
                dve.wait_ge(sb.bo_add, NCH * TPC)
                add_attention(0)
                dve_x(f, 0)
                dve_hidden(f, 0, range(HT), 0)

                def chunk(c, last=False, norm=True):
                    dve_hidden(f, c, range(0, 2), 1)
                    if not last:
                        add_attention(c + 1)
                    dve_hidden(f, c, range(2, 4), 1)
                    if norm:
                        normalize(c + 2)
                    dve_hidden(f, c, range(4, 6), 1)
                    if not last:
                        dve_x(f, c + 1)
                    dve_hidden(f, c, range(6, HT), 1)
                    dve_residual(f, c)
                    if not last:
                        dve_hidden(f, c + 1, range(HT), 0)

                chunk(0)
                with dve.Fori(1, NCH - 2) as c:
                    chunk(c)
                chunk(NCH - 2, norm=False)
                chunk(NCH - 1, last=True, norm=False)

            @block.scalar
            def _(act):
                act_x(f, 0)
                act_hidden(f, 0, range(HT), 0)

                def chunk(c, last=False):
                    act_hidden(f, c, range(0, 2), 1)
                    if not last:
                        act_ln_sqrt(ln3, c + 1)
                    act_hidden(f, c, range(2, 6), 1)
                    if not last:
                        act_x(f, c + 1)
                    act_hidden(f, c, range(6, HT), 1)
                    if not last:
                        act_hidden(f, c + 1, range(HT), 0)

                chunk(0)
                with act.Fori(1, NCH - 1) as c:
                    chunk(c)
                chunk(NCH - 1, last=True)

            @block.tensor
            def _(pe):
                def turn(c):
                    wait(pe, ln3.sem.xn, c + 1)
                    wait(pe, f.sem.xl, c)
                    pe_transpose(ln3, f.tr, f.sem.t_ps)

                def l0_free(c):
                    def free(m):
                        if m >= 4:
                            wait(pe, f.sem.l0_lo, c * HT + m - 3)
                        elif not (isinstance(c, int) and c == 0):
                            wait(pe, f.sem.l1_lo, (c - 1) * HT + 5 + m)
                        elif m < ST_BANKS:
                            wait(pe, sb.exp_done, BODIES * EXPS)
                        else:
                            wait(pe, sb.ctx_done, BATCH * PAIRS * QCH)
                    return free

                def l1_free(c):
                    def free(m):
                        if m == 0:
                            wait(pe, f.sem.l0_lo, c * HT + 5)
                        elif m >= 4:
                            wait(pe, f.sem.l1_lo, c * HT + m - 3)
                    return free

                def chunk(c, first=False, last=False):
                    pe_l1(f, c, range(0, 2), l1_free(c))
                    if not last:
                        pe_out_proj(pe, c + 1, lambda j: wait(pe, se.x2, j + 1) if first else wait(pe, f.sem.res, c * 2 + j - 1))
                    pe_l1(f, c, range(2, 6), l1_free(c))
                    if not last:
                        turn(c + 1)
                    pe_l1(f, c, range(6, HT), l1_free(c))
                    pe_l2(f, c, lambda j: wait(pe, f.sem.res, c * 2 + j - 1) if last else wait(pe, se.x2, c * 2 + j + 3))
                    if not last:
                        pe_l0(f, c + 1, l0_free(c + 1))

                turn(0)
                pe_l0(f, 0, l0_free(0))
                chunk(0, first=True)
                with pe.Fori(1, NCH - 1) as c:
                    chunk(c)
                chunk(NCH - 1, last=True)


_INS = ["L0_attn_x", "L0_attn_w_q", "L0_attn_w_k", "L0_attn_w_v", "L0_attn_w_o", "L0_attn_b_o",
        "L0_ffn_k0", "L0_ffn_k1", "L0_ffn_k2", "L0_ffn_s0", "L0_ffn_s1", "L0_ffn_s2"]


def kernel(**inputs):
    import numpy as np
    import concourse.bacc as bacc
    from concourse.bass_utils import run_bass_kernel_spmd

    nc = bacc.Bacc("TRN2", target_bir_lowering=False, num_devices=1)
    arrays, args = {}, []
    for name in _INS:
        a = np.ascontiguousarray(inputs[name])
        if a.ndim == 0:
            a = a.reshape(1)
        arrays[name] = a
        args.append(nc.dram_tensor(name, a.shape, U8 if a.dtype == np.bool_ else F32, kind="ExternalInput").ap())
    shape = arrays["L0_attn_x"].shape
    args.append(nc.dram_tensor("out", shape, F32, kind="ExternalOutput").ap())
    build(nc, *args)
    result = run_bass_kernel_spmd(nc, [arrays], core_ids=[0])
    return result.results[0]["out"]
```

```python
from contextlib import ExitStack

import concourse.bass as bass
from concourse import mybir

F32 = mybir.dt.float32
F16 = mybir.dt.float16
U8 = mybir.dt.uint8
U32 = mybir.dt.uint32
ALU = mybir.AluOpType
ACT = mybir.ActivationFunctionType
AX = mybir.AxisListType
RMAX = bass.bass_isa.ReduceOp.max

P = 128
BATCH, SEQ, D = 2, 2048, 256
HEADS, DK = 16, 16
HID = 1024
TOK = BATCH * SEQ
CH = 512
NCH = TOK // CH
TPC = CH // P
DT = D // P
HT = HID // P
EPS = 1e-5

X_SCALE = 2.0 ** 8
W0_SCALE = 2.0 ** -4
W1_SCALE = 2.0 ** -8
FFN_UNSCALE = 1.0 / (X_SCALE * W0_SCALE * W1_SCALE)
QK_SCALE = 2.0 ** 3
M_SCALE = 2.0 ** 13
MASK_A, MASK_B = 2.0 ** 15, -60000.0

PAIRS = HEADS // 2
BODY_PAIRS = 2
BODIES = BATCH * PAIRS // BODY_PAIRS
QCH = SEQ // CH
QT = SEQ // P
STEPS = sum(2 * i + 2 for i in range(QCH))
UNITS = sum(TPC * (i + 1) for i in range(QCH))
LEAD = 21
S_USES = UNITS + QCH
ST_BANKS, P_SLOTS = 3, 4
PV_LAG = 3
PV_POINTS = (3, 1, 2, 1, 1, 0, 2, 1, 2, 1, 3, 2, 2, 1, 1, 0, 1, 2, 2, 2)
TURN_DELAY = (2, 7, 3)
OWN_POINTS = (1, 2, 3, 8, 9, 12, 13, 15, 15, 16, 19, 21, 22, 25, 27, 28, 29, 31, 33, 34, 39)
AHEAD_POINTS = (39, 41, 41, 44, 46, 47, 51, 52, 52, 54, 56, 57, 59, 62, 63, 66, 68, 68, 71, 73, 75, 77, 77)


class LayerNormSems:

    def __init__(self, new):
        self.gate = new("gate")
        self.stat = new("stat")
        self.mv = new("mv")
        self.ve = new("ve")
        self.sd = new("sd")
        self.step = new("step")
        self.rstd = new("rstd")
        self.xn = new("xn")


class FfnSems:

    def __init__(self, new):
        self.t_ps = new("t_ps")
        self.xh = new("xh")
        self.xl = new("xl")
        self.l0_ps = new("l0_ps")
        self.l0_hi = new("l0_hi")
        self.l0_lo = new("l0_lo")
        self.l1_ps = new("l1_ps")
        self.l1_hi = new("l1_hi")
        self.l1_lo = new("l1_lo")
        self.l2_ps = new("l2_ps")
        self.res = new("res")


class PhaseASems:

    def __init__(self, new):
        self.x_in = new("x_in")
        self.k0_in = new("k0_in")
        self.k1_in = new("k1_in")
        self.k2_in = new("k2_in")
        self.w_in = new("w_in")
        self.s_in = new("s_in")
        self.bo_in = new("bo_in")
        self.zero = new("zero")
        self.consts = new("consts")
        self.vones = new("vones")
        self.sgn = new("sgn")
        self.sprep = new("sprep")
        self.w0d = new("w0d")
        self.w0 = new("w0")
        self.w1 = new("w1")
        self.w2 = new("w2")
        self.wmax = new("wmax")
        self.wamax = new("wamax")
        self.wchain = new("wchain")
        self.wscale = new("wscale")
        self.wt_ps = new("wt_ps")
        self.wt = new("wt")
        self.t2_ps = new("t2_ps")
        self.x2_t = new("x2_t")
        self.qk_ps = new("qk_ps")
        self.qk_hi = new("qk_hi")
        self.qk_lo = new("qk_lo")
        self.v_ps = new("v_ps")
        self.v_ev = new("v_ev")
        self.qk_st = new("qk_st")
        self.v_st = new("v_st")
        self.gate = new("gate")


class PhaseBSems:

    def __init__(self, new):
        self.rows_zero = new("rows_zero")
        self.rows_const = new("rows_const")
        self.qk_in0 = new("qk_in0")
        self.qk_in1 = new("qk_in1")
        self.v_in0 = new("v_in0")
        self.v_in1 = new("v_in1")
        self.s_ready = new("s_ready")
        self.s_done = new("s_done")
        self.m_neg = new("m_neg")
        self.m_hi = new("m_hi")
        self.m_cols = new("m_cols")
        self.rows_in = new("rows_in")
        self.st_ready = new("st_ready")
        self.exp_done = new("exp_done")
        self.mask_done = new("mask_done")
        self.pv_done = new("pv_done")
        self.ctx_done = new("ctx_done")
        self.ctx_st0 = new("ctx_st0")
        self.ctx_st1 = new("ctx_st1")
        self.gate_pe = new("gate_pe")
        self.gate_pool = new("gate_pool")
        self.bo_add = new("bo_add")


class PhaseCSems:

    def __init__(self, new):
        self.ctx_in = new("ctx_in")
        self.ctx_sum = new("ctx_sum")
        self.wgt_sum = new("wgt_sum")
        self.wgt_inv = new("wgt_inv")
        self.ctx_n = new("ctx_n")
        self.o_ps = new("o_ps")
        self.x2 = new("x2")
        self.out_st = new("out_st")
        self.gate = new("gate")


class LayerNormBuffers:
    def __init__(self, sbuf, sems):
        self.bn = sbuf("bn", [P, TPC, 6], F32)
        self.mv = sbuf("mv", [P, TPC, 2], F32)
        self.ve = sbuf("ve", [P, TPC], F32)
        self.sd = sbuf("sd", [P, TPC], F32)
        self.rs = sbuf("rs", [P, TPC], F32)
        self.nt = sbuf("nt", [P, TPC], F32)
        self.rstd = sbuf("rstd", [P, TPC], F32)
        self.xn = sbuf("xn", [P, TPC, D], F32)
        self.sem = sems


class FfnBuffers:
    def __init__(self, sbuf, psum, sems):
        self.xh = sbuf("xh", [P, DT, CH], F16)
        self.xl = sbuf("xl", [P, DT, CH], F16)
        self.h1h = sbuf("h1h", [P, HT, CH], F16)
        self.h1l = sbuf("h1l", [P, HT, CH], F16)
        self.h2h = sbuf("h2h", [P, HT, CH], F16)
        self.h2l = sbuf("h2l", [P, HT, CH], F16)
        self.mm = psum("mm", [P, 4, CH])
        self.acc = psum("acc", [P, 2, 2 * D])
        self.tr = psum("tr", [P, DT, CH])
        self.sem = sems


def wait(eng, sem, value):
    if not isinstance(value, int) or value > 0:
        eng.wait_ge(sem, value)


def build(nc, x, w_q, w_k, w_v, w_o, b_o, k0, k1, k2, s0, s1, s2, out):
    x_chunks = x.rearrange("b (c t p) d -> (b c) p t d", t=TPC, p=P)
    out_chunks = out.rearrange("b (c t p) d -> (b c) p t d", t=TPC, p=P)
    qk_scr = nc.dram_tensor("qk_scr", (2, 2, BATCH * PAIRS * 2 * DK, SEQ), F16).ap()
    v_scr = nc.dram_tensor("v_scr", (BATCH * PAIRS, SEQ, 64), F32).ap()
    ctx_scr = nc.dram_tensor("ctx_scr", (BATCH * PAIRS, P, SEQ), F32).ap()

    with ExitStack() as top:
        def sbuf(stack, name, shape, dt):
            return stack.enter_context(nc.sbuf_tensor(name, shape, dt))

        def psum(stack, name, shape):
            return stack.enter_context(nc.psum_tensor(name, shape, F32))

        def sem(stack, prefix):
            return lambda name: stack.enter_context(nc.semaphore(prefix + name))

        x_res = sbuf(top, "x_res", [P, NCH * TPC, D], F32)
        w0 = sbuf(top, "w0", [P, DT, HID], F16)
        w1 = sbuf(top, "w1", [P, HT, HID], F16)
        w2 = sbuf(top, "w2", [P, HT, D], F16)
        w_t = sbuf(top, "w_t", [P, 4, DT, D], F32)
        bo_row = sbuf(top, "bo_row", [P, D], F32)
        ident = sbuf(top, "ident", [P, P], F32)
        ident_h = sbuf(top, "ident_h", [P, P], F16)
        ident_mask = sbuf(top, "ident_mask", [P, P], F16)
        mask = sbuf(top, "mask", [P, P], F16)
        ffn_scale = sbuf(top, "ffn_scale", [P, 1], F32)
        qk_scale = sbuf(top, "qk_scale", [P, 2], F32)
        exp_scale = sbuf(top, "exp_scale", [P, 1], F32)

        proj_in = sbuf(top, "proj_in", [P, DT, CH], F32)
        qk_buf = [sbuf(top, f"qk{u}", [P, 4, SEQ], F16) for u in range(2)]
        v_buf = [sbuf(top, f"v{u}", [P, QT, 64], F32) for u in range(2)]
        m_part = [sbuf(top, f"m_part{u}", [P, QT, 2, QCH], F32) for u in range(2)]
        m_neg = sbuf(top, "m_neg", [P, 2, TPC], F32)
        m_col = sbuf(top, "m_col", [P, 2, 2, TPC], F16)
        m_row = sbuf(top, "m_row", [4 * TPC, P], F16)
        HEAD_ROWS = (slice(0, 64), slice(64, 128))
        SHIFT_ROWS = (slice(64, 66), slice(0, 2))
        ALL_ROWS = (slice(0, 66), slice(0, 128))

        def load_pair(sp, u, pair):
            for h in range(2):
                for g in range(4):
                    rows = slice(h * 64 + g * DK, h * 64 + (g + 1) * DK)
                    src = bass.ds(pair * 2 * DK + h * DK, DK)
                    sp.dma_start(q_part(u, h, rows, slice(0, SEQ)), qk_scr[g // 2, 0, src, :]).then_inc(qk_in[u], 16)
                    sp.dma_start(k_part(u, h, rows, slice(0, SEQ)), qk_scr[g % 2, 1, src, :]).then_inc(qk_in[u], 16)
            sp.dma_start(v_buf[u][:, :, :], v_scr[bass.ds(pair, 1)].rearrange("o (t p) e -> p (o t) e", p=P)).then_inc(v_in[u], 16)

        def k_part(u, h, rows, cols):
            return qk_buf[u][rows, h, cols]

        def q_part(u, h, rows, cols):
            return qk_buf[u][rows, 2 + h, cols]

        ffn_memory = {}

        def ffn_sbuf(n, shape, dt):
            if n not in ffn_memory:
                ffn_memory[n] = sbuf(top, "ffn_" + n, shape, dt)
            return ffn_memory[n]

        def ffn_psum(n, shape):
            if n not in ffn_memory:
                ffn_memory[n] = psum(top, "ffn_" + n, shape)
            return ffn_memory[n]

        def x_tile(c, t):
            return x_res[:, bass.ds(c * TPC + t, 1), :].rearrange("p o d -> p (o d)")

        def x_tiles(c, t, n):
            return x_res[:, bass.ds(c * TPC + t, n), :].rearrange("p o d -> p (o d)")

        def ln_buffers(name):
            return LayerNormBuffers(lambda n, shape, dt: sbuf(top, f"{name}_{n}", shape, dt), LayerNormSems(sem(top, name + "_")))

        def dve_ln_stats(ln, c):
            for t in range(TPC):
                nc.vector.bn_stats(ln.bn[:, t, :], x_tile(c, t)).then_inc(ln.sem.stat, 1)
            wait(nc.vector, ln.sem.stat, c * TPC + TPC)
            nc.vector.sem_inc(ln.sem.gate, 1)
            for t in range(TPC):
                nc.vector.bn_aggr(ln.mv[:, t, :], ln.bn[:, t, :]).then_inc(ln.sem.mv, 1)
            wait(nc.vector, ln.sem.mv, c * TPC + TPC)
            nc.vector.tensor_scalar(ln.ve[:, :], ln.mv[:, :, 1], EPS, None, ALU.add).then_inc(ln.sem.ve, 1)

        def act_ln_sqrt(ln, c):
            wait(nc.scalar, ln.sem.ve, c + 1)
            nc.scalar.activation(ln.sd[:, :], ln.ve[:, :], ACT.Sqrt).then_inc(ln.sem.sd, 1)

        def dve_ln_finish(ln, c, xn_read):
            wait(nc.vector, ln.sem.sd, c + 1)
            nc.vector.reciprocal(ln.rs[:, :], ln.sd[:, :]).then_inc(ln.sem.step, 1)
            wait(nc.vector, ln.sem.step, c * 4 + 1)
            nc.vector.tensor_tensor(ln.nt[:, :], ln.rs[:, :], ln.rs[:, :], ALU.mult).then_inc(ln.sem.step, 1)
            wait(nc.vector, ln.sem.step, c * 4 + 2)
            nc.vector.tensor_tensor(ln.sd[:, :], ln.nt[:, :], ln.ve[:, :], ALU.mult).then_inc(ln.sem.step, 1)
            wait(nc.vector, ln.sem.step, c * 4 + 3)
            nc.vector.tensor_scalar(ln.nt[:, :], ln.sd[:, :], -0.5, 1.5, ALU.mult, ALU.add).then_inc(ln.sem.step, 1)
            wait(nc.vector, ln.sem.step, c * 4 + 4)
            nc.vector.tensor_tensor(ln.rstd[:, :], ln.rs[:, :], ln.nt[:, :], ALU.mult).then_inc(ln.sem.rstd, 1)
            wait(nc.vector, ln.sem.rstd, c + 1)
            wait(nc.vector, xn_read, c)
            for t in range(TPC):
                ins = nc.vector.tensor_scalar(ln.xn[:, t, :], x_tile(c, t), ln.mv[:, t, 0:1], ln.rstd[:, t:t + 1],
                                              ALU.subtract, ALU.mult)
            ins.then_inc(ln.sem.xn, 1)

        def pe_transpose(ln, ps, done):
            for kt in range(DT):
                for t in range(TPC):
                    ins = nc.tensor.transpose(ps[:, kt, t * P:(t + 1) * P], ln.xn[:, t, kt * P:(kt + 1) * P], ident[:, :])
            ins.then_inc(done, 1)

        def ffn_buffers(name):
            return FfnBuffers(ffn_sbuf, ffn_psum, FfnSems(sem(top, name + "_")))

        def pe_l0(f, c, free):
            wait(nc.tensor, f.sem.xl, c + 1)
            for m in range(HT):
                free(m)
                for kt in range(DT):
                    for part in (f.xh, f.xl):
                        ins = nc.tensor.matmul(f.mm[:, m % 4, :], w0[:, kt, m * P:(m + 1) * P], part[:, kt, :],
                                               start=(kt == 0 and part is f.xh), stop=(kt == DT - 1 and part is f.xl))
                ins.then_inc(f.sem.l0_ps, 1)

        def pe_l1(f, c, ms, free, fill=None):
            for m in ms:
                free(m)
                for kt in range(HT):
                    if m == 0:
                        wait(nc.tensor, f.sem.l0_lo, c * HT + kt + 1)
                    for part in (f.h1h, f.h1l):
                        ins = nc.tensor.matmul(f.mm[:, m % 4, :], w1[:, kt, m * P:(m + 1) * P], part[:, kt, :],
                                               start=(kt == 0 and part is f.h1h), stop=(kt == HT - 1 and part is f.h1l))
                    if kt == HT - 1:
                        ins.then_inc(f.sem.l1_ps, 1)
                    if fill and kt % (HT // 2) == HT // 2 - 1:
                        fill()

        def pe_l2(f, c, free, fill=None):
            for t in range(TPC):
                if t % 2 == 0:
                    free(t // 2)
                for kt in range(HT):
                    if t == 0:
                        wait(nc.tensor, f.sem.l1_lo, c * HT + kt + 1)
                    for part in (f.h2h, f.h2l):
                        ins = nc.tensor.matmul(f.acc[:, t // 2, t % 2 * D:(t % 2 + 1) * D], part[:, kt, t * P:(t + 1) * P],
                                               w2[:, kt, :], start=(kt == 0 and part is f.h2h),
                                               stop=(kt == HT - 1 and part is f.h2l))
                if t % 2 == 1:
                    ins.then_inc(f.sem.l2_ps, 1)
                if fill and t < TPC - 1:
                    fill()

        def act_x(f, c):
            wait(nc.scalar, f.sem.t_ps, c + 1)
            wait(nc.scalar, f.sem.l0_ps, c * HT)
            nc.scalar.activation(f.xh[:, :, :], f.tr[:, :, :], ACT.Copy, scale=X_SCALE).then_inc(f.sem.xh, 1)

        def dve_x(f, c):
            wait(nc.vector, f.sem.xh, c + 1)
            for kt in range(DT):
                ins = nc.vector.scalar_tensor_tensor(out=f.xl[:, kt, :], in0=f.tr[:, kt, :], scalar=X_SCALE,
                                                     in1=f.xh[:, kt, :], op0=ALU.mult, op1=ALU.subtract)
            ins.then_inc(f.sem.xl, 1)

        def act_hidden(f, c, ms, layer):
            ps, hi, dst = ((f.sem.l0_ps, f.sem.l0_hi, f.h1h), (f.sem.l1_ps, f.sem.l1_hi, f.h2h))[layer]
            for m in ms:
                if m == 0:
                    if layer == 0:
                        wait(nc.scalar, f.sem.l1_ps, c * HT)
                    else:
                        wait(nc.scalar, f.sem.l2_ps, c * 2)
                wait(nc.scalar, ps, c * HT + m + 1)
                nc.scalar.activation(dst[:, m, :], f.mm[:, m % 4, :], ACT.Relu).then_inc(hi, 1)

        def dve_hidden(f, c, ms, layer):
            hi, lo, src, dst = ((f.sem.l0_hi, f.sem.l0_lo, f.h1h, f.h1l), (f.sem.l1_hi, f.sem.l1_lo, f.h2h, f.h2l))[layer]
            for m in ms:
                wait(nc.vector, hi, c * HT + m + 1)
                nc.vector.scalar_tensor_tensor(out=dst[:, m, :], in0=f.mm[:, m % 4, :], scalar=0.0, in1=src[:, m, :],
                                               op0=ALU.max, op1=ALU.subtract).then_inc(lo, 1)

        def dve_residual(f, c, js=range(2)):
            for j in js:
                wait(nc.vector, f.sem.l2_ps, c * 2 + j + 1)
                nc.vector.scalar_tensor_tensor(out=x_tiles(c, 2 * j, 2), in0=f.acc[:, j, :], scalar=ffn_scale[:, 0:1],
                                               in1=x_tiles(c, 2 * j, 2), op0=ALU.mult, op1=ALU.add).then_inc(f.sem.res, 1)

        ln1, ln2, ln3 = ln_buffers("ln1"), ln_buffers("ln2"), ln_buffers("ln3")
        fa, fc = ffn_buffers("a"), ffn_buffers("c")
        sa, sb, sc = PhaseASems(sem(top, "a_")), PhaseBSems(sem(top, "b_")), PhaseCSems(sem(top, "c_"))
        qk_in, v_in = (sb.qk_in0, sb.qk_in1), (sb.v_in0, sb.v_in1)
        block = top.enter_context(nc.Block())

        ctx_in = qk_buf[0][:, 0:2, :].bitcast(F32).rearrange("p a (t n) -> p a t n", t=DT)
        wgt_in = qk_buf[0][:, 2:4, :].bitcast(F32).rearrange("p a (t n) -> p a t n", t=DT)

        def load_ctx(sp, b, i):
            for a in range(2):
                for hf in range(DT):
                    src = ctx_scr.rearrange("(b q) (h a e) n -> b a (q h) e n", b=BATCH, h=2, a=2)[
                        bass.ds(b, 1), a, hf * 8:(hf + 1) * 8, :, bass.ds(i * CH, CH)].rearrange("o g e n -> (o g) e n")
                    for dst, e in ((ctx_in, 0), (wgt_in, DK)):
                        sp.dma_start(dst[:, a, hf, :], src[:, e:e + DK, :]).then_inc(sc.ctx_in, 16)

        def pe_out_proj(pe, c, free):
            wait(pe, sc.ctx_n, c + 1)
            for t in range(TPC):
                if t % 2 == 0:
                    free(t // 2)
                for kt in range(DT):
                    ins = nc.tensor.matmul(fc.acc[:, t // 2, t % 2 * D:(t % 2 + 1) * D], proj_in[:, kt, t * P:(t + 1) * P],
                                           w_t[:, 3, kt, :], start=(kt == 0), stop=(kt == DT - 1))
                if t % 2 == 1:
                    ins.then_inc(sc.o_ps, 1)

        units = [("unit", t, r) for i in range(QCH) for t in range(TPC * i, TPC * i + TPC) for r in range(i + 1)]
        last_unit = {i: max(n for n, x in enumerate(units) if x[1] // TPC == i) for i in range(QCH)}

        def with_turns(lo, hi):
            seq = []
            for n in range(lo, hi):
                seq.append(units[n])
                seq += [("turn", i) for i in range(QCH - 1) if last_unit[i] + TURN_DELAY[i] == n]
            return seq

        AHEAD = with_turns(0, LEAD)
        OWN = with_turns(LEAD, UNITS) + [("turn", QCH - 1)]
        assert len(AHEAD) == len(AHEAD_POINTS) and len(OWN) == len(OWN_POINTS)
        assert len(AHEAD) + len(OWN) == S_USES and S_USES % 2 == 0

        chunk_of = [i for i in range(QCH) for _ in range(2 * i + 2)]
        first_step = [chunk_of.index(i) for i in range(QCH)]

        def step_slots(s):
            i = chunk_of[s]
            out = []
            for par in range(2):
                kb = 2 * (s - first_step[i]) + par
                c0 = max(0, (kb - TPC * i) * P)
                if kb == 1 and i == 0:
                    c0 = 0
                for h in range(2):
                    out.append((kb, h, c0))
            return out

        def schedule(u, last):
            plan = [[] for _ in range(4 * STEPS)]
            work = [(u, x) for x in OWN] + [(1 - u, x) for x in AHEAD]
            for use, ((buf, x), point) in enumerate(zip(work, OWN_POINTS + AHEAD_POINTS)):
                if buf == u or not last:
                    plan[point].append((buf, x, use))
            return plan

        def diagonal(s):
            return chunk_of[s] * TPC <= step_slots(s)[0][0]

        body_steps = [(u, s) for u in range(BODY_PAIRS) for s in range(STEPS)]
        LOAD_STEP = AHEAD_POINTS[0] // 4
        OUT_PROJ_STEP = STEPS - 6
        EXPS, NSTEP = 4 * len(body_steps), len(body_steps)

        def bank(k):
            return 1 if k == EXPS - 1 else k % ST_BANKS

        def bank_free(k):
            return next(n for n in range(k - 1, k - EXPS, -1) if bank(n % EXPS) == bank(k)) + 1

        EARLY = [0] * 15 + [1] * 3 + [0]
        EARLY_T2 = 4
        slots = EARLY + [n % 2 for n in range(len(EARLY), len(AHEAD))]
        s_ps = (fa.tr, fa.acc)

        def pe_item(u, x, slot, done, cols):
            wait(nc.tensor, sb.s_done, done)
            if x[0] == "unit":
                _, t, r = x
                i = t // TPC
                w = CH if r < i else (t % TPC + 1) * P
                nc.tensor.sem_inc(sb.gate_pe, 1)
                for h in range(2):
                    ins = nc.tensor.matmul(s_ps[slot][:, h, 0:w], q_part(u, h, HEAD_ROWS[h], slice(t * P, (t + 1) * P)),
                                           k_part(u, h, HEAD_ROWS[h], slice(r * CH, r * CH + w)), start=True, stop=(r < i))
                if r == i:
                    for h in range(2):
                        ins = nc.tensor.matmul(s_ps[slot][:, h, w - P:w], ident_mask[:, :], mask[:, :],
                                               start=False, stop=True)
            else:
                wait(nc.tensor, sb.m_cols, cols)
                ins = nc.tensor.matmul(s_ps[slot][0:4 * TPC, 0, 0:P], m_col.rearrange("p h a t -> p (h a t)"), ident_h[:, :],
                                       start=True, stop=True)
            ins.then_inc(sb.s_ready, 1)

        def dve_item(u, x, use, slot, chunks):
            wait(nc.vector, sb.s_ready, use + 1)
            if x[0] == "unit":
                _, t, r = x
                i = t // TPC
                w = CH if r < i else (t % TPC + 1) * P
                nc.vector.tensor_reduce(m_part[u][:, t, :, r], s_ps[slot][:, :, 0:w], AX.X, ALU.max).then_inc(sb.s_done, 1)
                if units.index(x) == last_unit[i]:
                    wait(nc.vector, sb.s_done, use + 1)
                    nc.vector.tensor_reduce(m_neg.rearrange("p h t -> p t h"), m_part[u][:, i * TPC:(i + 1) * TPC, :, 0:i + 1], AX.X,
                                            ALU.max, negate=True).then_inc(sb.m_neg, 1)
                    wait(nc.vector, sb.m_neg, chunks + 1)
                    nc.vector.tensor_scalar(m_col[:, :, 0, :], m_neg[:, :, :], 1.0 / M_SCALE, None,
                                            ALU.mult).then_inc(sb.m_hi, 1)
                    wait(nc.vector, sb.m_hi, chunks + 1)
                    nc.vector.scalar_tensor_tensor(out=m_col[:, :, 1, :], in0=m_neg[:, :, :], scalar=1.0 / M_SCALE,
                                                   in1=m_col[:, :, 0, :], op0=ALU.mult, op1=ALU.subtract).then_inc(sb.m_cols, 1)
            else:
                wait(nc.vector, sb.rows_in, chunks * 32)
                nc.vector.tensor_copy(m_row[:, :], s_ps[slot][0:4 * TPC, 0, 0:P]).then_inc(sb.s_done, 1)

        def sp_rows(sp, u, i, use):
            wait(sp, sb.s_done, use + 1)
            for h in range(2):
                sp.dma_start(q_part(u, h, SHIFT_ROWS[h], slice(i * CH, (i + 1) * CH)),
                             m_row[2 * TPC * h:2 * TPC * (h + 1), :]).then_inc(sb.rows_in, 16)

        def pe_early(n):
            before = max([m + 1 for m in range(n) if slots[m] == slots[n]], default=0)
            pe_item(0, AHEAD[n], slots[n], before, AHEAD[n][1] + 1)

        def dve_early(n):
            dve_item(0, AHEAD[n], n, slots[n], AHEAD[n][1] if AHEAD[n][0] == "turn" else AHEAD[n][1] // TPC)

        with ExitStack() as st:
            k0_u8 = sbuf(st, "k0_u8", [P, 2 * DT, HID], U8)
            k1_u8 = sbuf(st, "k1_u8", [P, HT, HID], U8)
            k2_u8 = sbuf(st, "k2_u8", [P, HT, D], U8)
            w_in = sbuf(st, "w_in", [P, 4, DT, D], F32)
            w_diff = sbuf(st, "w_diff", [P, DT, HID], F16)
            s_in = sbuf(st, "s_in", [P, 3], F32)
            sgn = sbuf(st, "sgn", [P, 3], F32)
            s_abs = sbuf(st, "s_abs", [P, 3], F32)
            s_prod = sbuf(st, "s_prod", [P, 2], F32)
            w0_mul = sbuf(st, "w0_mul", [P, 1], F32)
            w1_mul = sbuf(st, "w1_mul", [P, 1], F32)
            w1_add = sbuf(st, "w1_add", [P, 1], F32)
            w_max = sbuf(st, "w_max", [P, 2], F32)
            w_amax = sbuf(st, "w_amax", [P, 2], F32)
            w_lim = sbuf(st, "w_lim", [P, 2], F32)
            w_pow = sbuf(st, "w_pow", [P, 2], F32)
            w_inv = sbuf(st, "w_inv", [P, 2], F32)
            qk_hi = sbuf(st, "qk_hi", [P, 2 * DT, CH], F16)
            qk_lo = sbuf(st, "qk_lo", [P, 2 * DT, CH], F16)
            v_pad = sbuf(st, "v_pad", [P, TPC, HEADS, 32], F32)
            f = fa
            se = sa

            def pe_t1(c, first=False):
                wait(nc.tensor, ln1.sem.xn, c + 1)
                if first:
                    wait(nc.tensor, f.sem.xl, c)
                else:
                    wait(nc.tensor, se.x2_t, c - 1)
                pe_transpose(ln1, f.tr, f.sem.t_ps)

            def pe_t2(c, last=False):
                wait(nc.tensor, ln2.sem.xn, c + 1)
                if last:
                    wait(nc.tensor, sb.s_done, EARLY.index(1))
                else:
                    wait(nc.tensor, f.sem.xl, c + 2)
                pe_transpose(ln2, f.tr, se.t2_ps)

            def pe_qk(c, src, bank_free, fill=None):
                wait(nc.tensor, se.x2_t, c + 1)
                for j in range(2 * DT):
                    bank_free(j)
                    for kt in range(DT):
                        ins = nc.tensor.matmul(f.mm[:, j, :], w_t[:, j // DT, kt, j % DT * P:(j % DT + 1) * P],
                                               src[:, kt, :], start=(kt == 0), stop=(kt == DT - 1))
                    ins.then_inc(se.qk_ps, 1)
                    if fill:
                        fill()

            def pe_v(c, src, bank_free):
                for t in range(TPC):
                    if t % 2 == 0:
                        bank_free(t // 2)
                    for kt in range(DT):
                        ins = nc.tensor.matmul(f.acc[:, t // 2, t % 2 * D:(t % 2 + 1) * D], src[:, kt, t * P:(t + 1) * P],
                                               w_t[:, 2, kt, :], start=(kt == 0), stop=(kt == DT - 1))
                    if t % 2 == 1:
                        ins.then_inc(se.v_ps, 1)

            def act_x2(c, dst):
                wait(nc.scalar, se.t2_ps, c + 1)
                if dst is proj_in:
                    wait(nc.scalar, se.v_ps, c * 2)
                nc.scalar.activation(dst[:, :, :], f.tr[:, :, :], ACT.Copy).then_inc(se.x2_t, 1)

            def act_qk(c, js):
                for j in js:
                    if j == 0:
                        wait(nc.scalar, se.qk_st, c * 128)
                    wait(nc.scalar, se.qk_ps, c * 4 + j + 1)
                    nc.scalar.activation(qk_hi[:, j, :], f.mm[:, j, :], ACT.Copy,
                                         scale=qk_scale[:, j // DT:j // DT + 1]).then_inc(se.qk_hi, 1)

            def act_v(c):
                for j in range(2):
                    if j == 0:
                        wait(nc.scalar, se.v_st, c * 64)
                    wait(nc.scalar, se.v_ps, c * 2 + j + 1)
                    nc.scalar.activation(v_pad[:, 2 * j:2 * j + 2, :, 0:DK].rearrange("p t h d -> p (t h) d"),
                                         f.acc[:, j, :].rearrange("p (g d) -> p g d", d=DK),
                                         ACT.Copy).then_inc(se.v_ev, 1)

            proj_last = w_in[:, 0:DT, :, :].rearrange("p n t d -> p n (t d)")

            def dve_qk(c, js):
                for j in js:
                    wait(nc.vector, se.qk_hi, c * 4 + j + 1)
                    nc.vector.scalar_tensor_tensor(out=qk_lo[:, j, :], in0=f.mm[:, j, :],
                                                   scalar=qk_scale[:, j // DT:j // DT + 1], in1=qk_hi[:, j, :],
                                                   op0=ALU.mult, op1=ALU.subtract).then_inc(se.qk_lo, 1)

            @block.sync
            def _(sp):
                sp.dma_start(x_res[:, 0:TPC, :], x_chunks[0]).then_inc(se.x_in, 16)
                sp.dma_start(k0_u8[:, :, :], k0.rearrange("(t p) f -> p t f", p=P)).then_inc(se.k0_in, 16)
                for n, s in enumerate((s0, s1, s2)):
                    sp.dma_start(s_in[:, n:n + 1], s.rearrange("(a b) -> a b", a=1).to_broadcast([P, 1])).then_inc(se.s_in, 16)
                sp.dma_start(k1_u8[:, :, :], k1.rearrange("(t p) f -> p t f", p=P)).then_inc(se.k1_in, 16)
                for n, w in enumerate((w_q, w_k, w_v, w_o)):
                    sp.dma_start(w_in[:, n, :, :], w.rearrange("(t p) d -> p t d", p=P)).then_inc(se.w_in, 16)
                sp.dma_start(k2_u8[:, :, :], k2.rearrange("(t p) f -> p t f", p=P)).then_inc(se.k2_in, 16)
                sp.dma_start(bo_row[:, :], b_o.rearrange("(a d) -> a d", a=1).to_broadcast([P, D])).then_inc(se.bo_in, 16)
                with sp.Fori(1, NCH) as c:
                    wait(sp, se.x_in, c * 16)
                    sp.dma_start(x_res[:, bass.ds(c * TPC, TPC), :],
                                 x_chunks[bass.ds(c, 1)].rearrange("o p t d -> (o p) t d")).then_inc(se.x_in, 16)

                def store(b, i):
                    for n, part in enumerate((qk_hi, qk_lo)):
                        if n == 0:
                            wait(sp, se.qk_lo, b * (QCH * 4) + i * 4 + 4)
                        for j in range(2 * DT):
                            sp.dma_start(qk_scr[n, j // DT, b * D + j % DT * P:b * D + (j % DT + 1) * P, bass.ds(i * CH, CH)],
                                         part[:, j, :]).then_inc(se.qk_st, 16)
                    wait(sp, se.v_ev, b * (QCH * 2) + i * 2 + 2)
                    for t in range(TPC):
                        sp.dma_start(v_scr[b * PAIRS:(b + 1) * PAIRS, bass.ds(i * CH + t * P, P), :].rearrange("g p e -> p g e"),
                                     v_pad[:, t, :, :].rearrange("p (g h) e -> p g (h e)", h=2)).then_inc(se.v_st, 16)

                with sp.Fori(0, QCH) as i:
                    store(0, i)
                sp.wait_ge(se.qk_st, QCH * 128)
                sp.wait_ge(se.v_st, QCH * 64)
                sp.wait_ge(sb.rows_const, 4)
                load_pair(sp, 0, 0)
                with sp.Fori(0, QCH - 2) as i:
                    store(1, i)
                sp_rows(sp, 0, 0, AHEAD.index(("turn", 0)))
                store(1, QCH - 2)
                store(1, QCH - 1)

            @block.gpsimd
            def _(pool):
                nc.gpsimd.memset(ident[:, :], 0.0).then_inc(se.zero, 1)
                nc.gpsimd.memset(mask[:, :], 0.0).then_inc(se.zero, 1)
                nc.gpsimd.memset(v_pad[:, :, :, DK:32], 1.0).then_inc(se.vones, 1)
                pool.wait_ge(se.zero, 2)
                nc.gpsimd.affine_select(out=ident[:, :], in_=ident[:, :], compare_op=ALU.not_equal, fill=1.0, base=0,
                                        pattern=[[-1, P]], channel_multiplier=1).then_inc(se.consts, 1)
                nc.gpsimd.affine_select(out=mask[:, :], in_=mask[:, :], compare_op=ALU.is_ge, fill=MASK_B, base=0,
                                        pattern=[[-1, P]], channel_multiplier=1).then_inc(se.consts, 1)
                pool.wait_ge(se.consts, 2)
                nc.gpsimd.tensor_copy(ident_h[:, :], ident[:, :]).then_inc(se.consts, 1)
                nc.gpsimd.tensor_scalar(ident_mask[:, :], ident[:, :], MASK_A, 0.0, ALU.mult, ALU.add).then_inc(se.consts, 1)
                pool.wait_ge(se.k1_in, 16)
                pool.wait_ge(se.sprep, 3)
                for hf in range(2):
                    rows = slice(hf * HT // 2, (hf + 1) * HT // 2)
                    nc.gpsimd.tensor_scalar(w1[:, rows, :], k1_u8[:, rows, :], w1_mul[:, 0:1], w1_add[:, 0:1],
                                            ALU.mult, ALU.add).then_inc(se.w1, 1)
                pool.wait_ge(se.wmax, 2)
                nc.gpsimd.partition_all_reduce(w_amax[:, :], w_max[:, :], P, RMAX).then_inc(se.wamax, 1)
                pool.wait_ge(se.wamax, 1)
                for u in range(2):
                    nc.gpsimd.memset(k_part(u, 0, SHIFT_ROWS[0], slice(0, SEQ)), M_SCALE).then_inc(sb.rows_const, 1)
                    nc.gpsimd.memset(k_part(u, 1, slice(0, 64), slice(0, SEQ)), 0.0).then_inc(sb.rows_zero, 1)
                    nc.gpsimd.memset(q_part(u, 1, slice(0, 64), slice(0, SEQ)), 0.0).then_inc(sb.rows_zero, 1)
                pool.wait_ge(sb.rows_zero, 4)
                for u in range(2):
                    nc.gpsimd.memset(k_part(u, 1, SHIFT_ROWS[1], slice(0, SEQ)), M_SCALE).then_inc(sb.rows_const, 1)
                pool.wait_ge(se.bo_in, 16)
                with pool.Fori(0, NCH) as c:
                    pool.wait_ge(ln2.sem.xn, c + 1)
                    pool.sem_inc(sb.gate_pool, 1)
                    for t in range(TPC):
                        nc.gpsimd.tensor_tensor(x_tile(c, t), x_tile(c, t), bo_row[:, :], ALU.add).then_inc(sb.bo_add, 1)

            @block.vector
            def _(dve):
                dve.wait_ge(se.x_in, 16)
                dve_ln_stats(ln1, 0)
                dve.wait_ge(se.s_in, 48)
                nc.vector.tensor_scalar(sgn[:, :], s_in[:, :], 0.0, 2.0, ALU.is_ge, ALU.mult).then_inc(se.sgn, 1)
                dve.wait_ge(se.sgn, 1)
                nc.vector.tensor_scalar(s_abs[:, :], sgn[:, :], -1.0, None, ALU.add).then_inc(se.sgn, 1)
                dve.wait_ge(se.sgn, 2)
                nc.vector.tensor_scalar(w0_mul[:, :], s_abs[:, 0:1], 2.0 * W0_SCALE, None, ALU.mult).then_inc(se.sprep, 1)
                nc.vector.tensor_scalar(w1_mul[:, :], s_abs[:, 1:2], 2.0 * W1_SCALE, None, ALU.mult).then_inc(se.sprep, 1)
                nc.vector.tensor_scalar(w1_add[:, :], s_abs[:, 1:2], -W1_SCALE, None, ALU.mult).then_inc(se.sprep, 1)
                nc.vector.tensor_tensor(s_prod[:, :], s_abs[:, 0:2], s_in[:, 0:2], ALU.mult).then_inc(se.sgn, 1)
                dve_ln_finish(ln1, 0, f.sem.t_ps)
                dve.wait_ge(se.k0_in, 16)
                nc.vector.tensor_tensor(w_diff[:, :, :], k0_u8[:, 0:DT, :], k0_u8[:, DT:, :], ALU.subtract).then_inc(se.w0d, 1)
                dve.wait_ge(se.w0d, 1)
                dve.wait_ge(se.sprep, 1)
                nc.vector.tensor_scalar(w0[:, :, :], w_diff[:, :, :], w0_mul[:, 0:1], None, ALU.mult).then_inc(se.w0, 1)
                dve_x(f, 0)
                dve_hidden(f, 0, range(HT), 0)
                dve.wait_ge(se.sgn, 3)
                nc.vector.tensor_tensor(s_prod[:, 0:1], s_prod[:, 0:1], s_prod[:, 1:2], ALU.mult).then_inc(se.sgn, 1)
                dve.wait_ge(se.sgn, 4)
                nc.vector.tensor_scalar(ffn_scale[:, :], s_prod[:, 0:1], s_in[:, 2:3], 2.0 * FFN_UNSCALE,
                                        ALU.mult, ALU.mult).then_inc(se.sgn, 1)
                dve.wait_ge(se.k2_in, 16)
                nc.vector.tensor_scalar(w2[:, :, :], k2_u8[:, :, :], 2.0, -1.0, ALU.mult, ALU.add).then_inc(se.w2, 1)
                dve.wait_ge(se.w_in, 64)
                for n in range(2):
                    nc.vector.tensor_reduce(w_max[:, n:n + 1], w_in[:, n, :, :], AX.XY, ALU.max,
                                            apply_absolute_value=True).then_inc(se.wmax, 1)
                dve.wait_ge(se.x_in, 32)
                dve_ln_stats(ln1, 1)
                dve_ln_finish(ln1, 1, f.sem.t_ps)
                dve.wait_ge(se.wamax, 1)
                nc.vector.tensor_scalar(w_lim[:, :], w_amax[:, :], 2.0 ** -60, None, ALU.max).then_inc(se.wchain, 1)
                dve.wait_ge(se.wchain, 1)
                nc.vector.tensor_scalar(w_pow[:, :].bitcast(U32), w_lim[:, :].bitcast(U32), 0x7F800000, None,
                                        ALU.bitwise_and).then_inc(se.wchain, 1)
                dve.wait_ge(se.wchain, 2)
                nc.vector.reciprocal(w_inv[:, :], w_pow[:, :]).then_inc(se.wchain, 1)
                nc.vector.tensor_scalar(exp_scale[:, :], w_pow[:, 0:1], w_pow[:, 1:2],
                                        DK ** -0.5 / QK_SCALE ** 2, ALU.mult, ALU.mult).then_inc(se.wscale, 1)
                dve.wait_ge(se.wchain, 3)
                nc.vector.tensor_scalar(qk_scale[:, :], w_inv[:, :], QK_SCALE, None, ALU.mult).then_inc(se.wscale, 1)
                dve.wait_ge(se.sgn, 5)

                def chunk(c, first=False):
                    dve_hidden(f, c, range(0, 4), 1)
                    if not first:
                        dve_qk(c - 1, range(2 * DT))
                    dve_hidden(f, c, range(4, 6), 1)
                    dve_x(f, c + 1)
                    dve_hidden(f, c, range(6, HT), 1)
                    dve_residual(f, c)
                    dve_hidden(f, c + 1, range(HT), 0)
                    wait(dve, f.sem.res, c * 2 + 2)
                    dve.sem_inc(se.gate, 1)
                    dve_ln_stats(ln2, c)

                def next_ln(c):
                    wait(dve, se.x_in, (c + 3) * 16)
                    dve.sem_inc(se.gate, 1)
                    dve_ln_stats(ln1, c + 2)
                    dve_ln_finish(ln2, c, se.t2_ps)
                    dve_ln_finish(ln1, c + 2, f.sem.t_ps)

                chunk(0, first=True)
                next_ln(0)
                with dve.Fori(1, NCH - 2) as c:
                    chunk(c)
                    next_ln(c)
                chunk(NCH - 2)
                dve_ln_finish(ln2, NCH - 2, se.t2_ps)
                c = NCH - 1
                n = 0
                for m in range(HT):
                    if m in (0, 3):
                        dve_hidden(f, c, [m], 1)
                        continue
                    dve_early(n)
                    dve_early(n + 1)
                    n += 2
                    dve_hidden(f, c, [m], 1)
                dve_early(n)
                dve_early(n + 1)
                dve_residual(f, c, [0])
                dve_early(n + 2)
                dve_residual(f, c, [1])
                n += 3
                wait(dve, f.sem.res, c * 2 + 2)
                dve_ln_stats(ln2, c)
                dve_ln_finish(ln2, c, se.t2_ps)
                dve_qk(c - 1, range(2 * DT))
                for j in range(2 * DT):
                    dve_qk(c, [j])
                    dve_early(n + j)
                assert n + 2 * DT == len(EARLY)

            @block.scalar
            def _(act):
                act_ln_sqrt(ln1, 0)
                act_x(f, 0)
                for n in range(4):
                    act.wait_ge(se.wt_ps, n + 1)
                    nc.scalar.activation(w_t[:, n, :, :], f.mm[:, n, :].rearrange("p (t d) -> p t d", t=DT),
                                         ACT.Copy).then_inc(se.wt, 1)
                act_hidden(f, 0, range(HT), 0)
                act_ln_sqrt(ln1, 1)
                act.wait_ge(se.wscale, 2)
                act.wait_ge(se.vones, 1)

                def chunk(c, first=False):
                    act_hidden(f, c, range(0, 3), 1)
                    if not first:
                        act_x2(c - 1, proj_in)
                    act_hidden(f, c, range(3, 4), 1)
                    if not first:
                        act_qk(c - 1, range(2 * DT))
                        act_v(c - 1)
                    act_hidden(f, c, range(4, 6), 1)
                    act_x(f, c + 1)
                    act_hidden(f, c, range(6, HT), 1)
                    act_hidden(f, c + 1, range(HT), 0)
                    act_ln_sqrt(ln2, c)

                chunk(0, first=True)
                act_ln_sqrt(ln1, 2)
                chunk(1)
                act_ln_sqrt(ln1, 3)
                with act.Fori(2, NCH - 2) as c:
                    chunk(c)
                    act_ln_sqrt(ln1, c + 2)
                chunk(NCH - 2)
                c = NCH - 1
                act_hidden(f, c, range(0, 3), 1)
                act_x2(c - 1, proj_in)
                act_hidden(f, c, range(3, HT), 1)
                act_qk(c - 1, [0])
                act_ln_sqrt(ln2, c)
                act_qk(c - 1, range(1, 2 * DT))
                act_x2(c, proj_last)
                act_v(c - 1)
                act_qk(c, range(2 * DT))
                act_v(c)

            @block.tensor
            def _(pe):
                pe.wait_ge(se.consts, 2)
                pe_t1(0, first=True)
                pe.wait_ge(se.w_in, 64)
                for n in range(4):
                    for jt in range(DT):
                        for it in range(DT):
                            ins = nc.tensor.transpose(f.mm[:, n, it * D + jt * P:it * D + (jt + 1) * P],
                                                      w_in[:, n, jt, it * P:(it + 1) * P], ident[:, :])
                    ins.then_inc(se.wt_ps, 1)
                pe.wait_ge(se.w0, 1)

                def l0_free(c):
                    def free(m):
                        if m < 4 and isinstance(c, int) and c == 0:
                            wait(pe, se.wt, m + 1)
                        elif m < 4:
                            wait(pe, f.sem.l1_lo, (c - 1) * HT + 5 + m)
                        else:
                            wait(pe, f.sem.l0_lo, c * HT + m - 3)
                    return free

                def l1_free(c, first):
                    def free(m):
                        if m == 0:
                            wait(pe, f.sem.l0_lo, c * HT + 5)
                        elif m >= 4 and first:
                            wait(pe, f.sem.l1_lo, c * HT + m - 3)
                        elif m >= 4:
                            wait(pe, se.qk_lo, (c - 1) * 4 + m - 3)
                    return free

                def l2_free(c, first):
                    def free(j):
                        if first:
                            wait(pe, se.w2, 1)
                        else:
                            wait(pe, se.v_ev, (c - 1) * 2 + j + 1)
                    return free

                def qk_free(c):
                    return lambda j: wait(pe, f.sem.l1_lo, (c + 1) * HT + j + 1)

                def v_free(c):
                    return lambda j: wait(pe, f.sem.res, c * 2 + j + 1)

                def chunk(c, first=False):
                    pe_l1(f, c, range(0, 3), l1_free(c, first))
                    if not first:
                        pe_t2(c - 1)
                    pe_l1(f, c, range(3, 4), l1_free(c, first))
                    if not first:
                        pe_qk(c - 1, proj_in, qk_free(c - 1))
                        pe_v(c - 1, proj_in, v_free(c - 1))
                    pe_l1(f, c, range(4, 6), l1_free(c, first))
                    pe_t1(c + 1, first=first)
                    pe_l1(f, c, range(6, HT), l1_free(c, first))
                    pe_l2(f, c, l2_free(c, first))
                    pe_l0(f, c + 1, l0_free(c + 1))

                early = iter(range(len(EARLY)))

                def fill_early():
                    pe_early(next(early))

                pe_l0(f, 0, l0_free(0))
                pe.wait_ge(se.w1, 2)
                chunk(0, first=True)
                with pe.Fori(1, NCH - 1) as c:
                    chunk(c)
                pe.wait_ge(qk_in[0], 256)
                c = NCH - 1
                pe_l1(f, c, range(0, 1), l1_free(c, True))
                pe_l1(f, c, range(1, 3), l1_free(c, True), fill_early)
                wait(pe, sb.s_done, EARLY_T2)
                pe_t2(c - 1)
                pe_l1(f, c, range(3, 4), l1_free(c, True))
                wait(pe, se.x2_t, c)
                pe_l1(f, c, range(4, HT), l1_free(c, True), fill_early)
                pe_l2(f, c, v_free(c - 1), fill_early)
                pe_qk(c - 1, proj_in, lambda j: wait(pe, f.sem.l1_lo, c * HT + 5 + j))
                pe_t2(c, last=True)
                pe_v(c - 1, proj_in, v_free(c))
                wait(pe, se.v_ev, c * 2)
                pe_qk(c, proj_last, lambda j: wait(pe, se.qk_lo, (c - 1) * 4 + j + 1), fill_early)
                wait(pe, sb.s_done, len(EARLY) - 1)
                pe_v(c, proj_last, lambda j: None)

        with ExitStack() as st:
            probs = sbuf(st, "probs", [P, P_SLOTS, 4, CH], F32)
            ctx_out = sbuf(st, "ctx_out", [P, 2, CH], F32)
            st_ps = [fa.mm[:, n, :] for n in range(ST_BANKS)]
            ctx_ps = fa.mm[:, 3, :]
            se = sb
            ctx_st = (se.ctx_st0, se.ctx_st1)

            @block.sync
            def _(sp):
                def store(pair, n, i):
                    wait(sp, se.ctx_done, n + 1)
                    sp.dma_start(ctx_scr[bass.ds(pair, 1), :, i * CH:(i + 1) * CH].rearrange("o p n -> (o p) n"),
                                 ctx_out[:, i % 2, :]).then_inc(ctx_st[i % 2], 16)

                def body(it, last):
                    for u in range(BODY_PAIRS):
                        pair = it * BODY_PAIRS + u
                        base = pair * S_USES + len(AHEAD)
                        turns = [(b, x[1], use) for step in schedule(u, last and u == 1) for b, x, use in step if x[0] == "turn"]
                        order = [turns[0], "load", 0, 1, turns[1]] + turns[2:3] + [2] + turns[3:4] + [3]
                        for x in order:
                            if x == "load":
                                wait(sp, se.pv_done, pair * STEPS)
                                if last and u == 1:
                                    load_ctx(sp, 0, 0)
                                else:
                                    load_pair(sp, 1 - u, pair + 1)
                                continue
                            if last and u == 1 and x == QCH - 2:
                                wait(sp, sc.ctx_n, 1)
                                load_ctx(sp, 0, 1)
                            if isinstance(x, int):
                                store(pair, pair * QCH + x, x)
                            else:
                                sp_rows(sp, x[0], x[1], base + x[2])

                sp_rows(sp, 0, 1, AHEAD.index(("turn", 1)))
                sp.wait_ge(sa.qk_st, NCH * 128)
                sp.wait_ge(sa.v_st, NCH * 64)
                body(0, False)
                with sp.Fori(1, BODIES - 1) as it:
                    body(it, False)
                body(BODIES - 1, True)
                for sem in ctx_st:
                    sp.wait_ge(sem, 8 * BATCH * PAIRS * QCH)

            @block.gpsimd
            def _(pool):
                def body(it):
                    for g, (u, s) in enumerate(body_steps):
                        if not diagonal(s):
                            continue
                        i = chunk_of[s]
                        for par in range(2):
                            kb, _, c0 = step_slots(s)[2 * par]
                            w = (kb - TPC * i + 1) * P - c0
                            pool.wait_ge(se.exp_done, it * EXPS + 4 * g + 2 * par + 2)
                            pool.sem_inc(se.gate_pool, 1)
                            view = probs[:, g % P_SLOTS, 2 * par:2 * par + 2, c0:c0 + w]
                            nc.gpsimd.affine_select(out=view, in_=view, compare_op=ALU.is_ge, fill=0.0,
                                                    base=c0 - (kb - TPC * i) * P, pattern=[[0, 2], [1, w]],
                                                    channel_multiplier=-1).then_inc(se.mask_done, 1)

                with pool.Fori(0, BODIES - 1) as it:
                    body(it)
                body(BODIES - 1)

            @block.vector
            def _(dve):
                for n in range(len(EARLY), len(AHEAD)):
                    dve_early(n)

                def body(it, last):
                    for u in range(BODY_PAIRS):
                        pair = it * BODY_PAIRS + u
                        for step in schedule(u, last and u == 1):
                            for buf, x, use in step:
                                i = x[1] if x[0] == "turn" else x[1] // TPC
                                owner = pair if buf == u else pair + 1
                                dve_item(buf, x, pair * S_USES + len(AHEAD) + use, (len(AHEAD) + use) % 2, owner * QCH + i)

                with dve.Fori(0, BODIES - 1) as it:
                    body(it, False)
                body(BODIES - 1, True)

            @block.scalar
            def _(act):
                ends = [g + PV_LAG for g, (u, s) in enumerate(body_steps) if s + 1 == STEPS or chunk_of[s + 1] != chunk_of[s]]

                def body(it, first=False, last=False):
                    def evacuate(n, body=0):
                        stored = BODY_PAIRS * QCH * 8
                        wait(act, se.pv_done, it * NSTEP + (body * NSTEP + ends[n] - PV_LAG + 1))
                        wait(act, ctx_st[n % 2], it * stored + (body * stored + n // 2 * 16))
                        nc.scalar.activation(ctx_out[:, n % 2, :], ctx_ps[:, :], ACT.Copy).then_inc(se.ctx_done, 1)

                    for g, (u, s) in enumerate(body_steps):
                        for j, (kb, h, c0) in enumerate(step_slots(s)):
                            k = 4 * g + j
                            if first and k == 4 * (P_SLOTS - 1):
                                act.wait_ge(sa.qk_st, NCH * 128)
                                act.wait_ge(sa.v_st, NCH * 64)
                            if j == 0:
                                wait(act, se.pv_done, it * NSTEP + (g - P_SLOTS + 1))
                            wait(act, se.st_ready, it * EXPS + k + 1)
                            nc.scalar.activation(probs[:, g % P_SLOTS, j, c0:CH], st_ps[bank(k)][:, c0:CH], ACT.Exp,
                                                 scale=exp_scale[:, 0:1]).then_inc(se.exp_done, 1)
                            if j == PV_POINTS[s] and g in ends:
                                evacuate(ends.index(g))
                            if j == PV_POINTS[s] and g + NSTEP in ends and not first:
                                evacuate(ends.index(g + NSTEP), -1)
                    if last:
                        act_ln_sqrt(ln3, 0)
                        for n, g in enumerate(ends):
                            if g >= NSTEP:
                                evacuate(n)

                body(0, first=True)
                with act.Fori(1, BODIES - 1) as it:
                    body(it)
                body(BODIES - 1, last=True)

            @block.tensor
            def _(pe):
                def load_wait(u, it):
                    pe.wait_ge(qk_in[u], (it + 1) * 256)
                    pe.sem_inc(sb.gate_pe, 1)

                for n in range(len(EARLY), len(AHEAD)):
                    if n == len(EARLY):
                        pe.wait_ge(sa.v_ev, NCH * 2)
                    pe_early(n)
                pe.wait_ge(sa.qk_lo, NCH * 4)

                def body(it, first=False, last=False):
                    def scores(g, j):
                        u, s = body_steps[g]
                        i = chunk_of[s]
                        kb, h, c0 = step_slots(s)[j]
                        k = 4 * g + j
                        if j == 0 and s == first_step[i]:
                            wait(pe, se.rows_in, (it * BODY_PAIRS + u) * (QCH * 32) + (i + 1) * 32)
                        wait(pe, se.exp_done, it * EXPS + bank_free(k))
                        rows = ALL_ROWS[h]
                        nc.tensor.matmul(st_ps[bank(k)][:, c0:CH], k_part(u, h, rows, slice(kb * P, (kb + 1) * P)),
                                         q_part(u, h, rows, slice(i * CH + c0, (i + 1) * CH)), start=True, stop=True).then_inc(se.st_ready, 1)

                    def products(g, body=0):
                        u, s = body_steps[g]
                        pair = it * BODY_PAIRS + (body * BODY_PAIRS + u)
                        i = chunk_of[s]
                        start = s == first_step[i]
                        final = s + 1 == STEPS or chunk_of[s + 1] != i
                        if s == 0:
                            wait(pe, v_in[u], (it + 1) * 16)
                        if start:
                            wait(pe, se.ctx_done, pair * QCH + i)
                        if diagonal(s):
                            wait(pe, se.mask_done, pair * (QCH * TPC) + i * TPC + 2 * (s - first_step[i] - 2 * i) + 2)
                        wait(pe, se.exp_done, it * EXPS + (body * EXPS + 4 * g + 4))
                        for j, (kb, h, c0) in enumerate(step_slots(s)):
                            row = 32 * (2 * h + kb % 2)
                            ins = nc.tensor.matmul(ctx_ps[row:row + 32, c0:CH], v_buf[u][:, kb, h * 32:(h + 1) * 32],
                                                   probs[:, g % P_SLOTS, j, c0:CH], start=start, stop=final,
                                                   tile_position=(0, row))
                        ins.then_inc(se.pv_done, 1)

                    plans = [schedule(u, last and u == 1) for u in range(BODY_PAIRS)]
                    for g, (u, s) in enumerate(body_steps):
                        pair = it * BODY_PAIRS + u
                        if s == LOAD_STEP and not (last and u == 1):
                            load_wait(1 - u, it + u)
                        for j in range(4):
                            scores(g, j)
                            if j == PV_POINTS[s] and g >= PV_LAG:
                                products(g - PV_LAG)
                            elif j == PV_POINTS[s] and not first:
                                products(g - PV_LAG + NSTEP, -1)
                            for b, x, use in plans[u][4 * s + j]:
                                owner = pair if b == u else pair + 1
                                cols = owner * QCH + x[1] + 1 if x[0] == "turn" else None
                                pe_item(b, x, (len(AHEAD) + use) % 2, pair * S_USES + (len(AHEAD) + use - 1), cols)
                        if last and u == 1 and s == OUT_PROJ_STEP:
                            wait(pe, se.s_done, BATCH * PAIRS * S_USES)
                            pe_out_proj(pe, 0, lambda j: None)
                    if last:
                        for g in range(NSTEP - PV_LAG, NSTEP):
                            products(g)

                body(0, first=True)
                with pe.Fori(1, BODIES - 1) as it:
                    body(it)
                body(BODIES - 1, last=True)

        with ExitStack() as st:
            f = fc
            se = sc

            def load_done(c):
                return c * 128 + 128

            @block.sync
            def _(sp):
                with sp.Fori(2, NCH) as c:
                    wait(sp, se.ctx_n, c)
                    load_ctx(sp, c // QCH, c % QCH)
                with sp.Fori(0, NCH) as c:
                    wait(sp, f.sem.res, c * 2 + 2)
                    sp.dma_start(out_chunks[bass.ds(c, 1)].rearrange("o p t d -> (o p) t d"),
                                 x_res[:, bass.ds(c * TPC, TPC), :]).then_inc(se.out_st, 16)
                sp.wait_ge(se.out_st, NCH * 16)

            @block.vector
            def _(dve):
                def normalize(c):
                    wait(dve, se.ctx_in, load_done(c))
                    dve.sem_inc(se.gate, 1)
                    nc.vector.tensor_tensor(wgt_in[:, 0, :, :], wgt_in[:, 0, :, :], wgt_in[:, 1, :, :], ALU.add).then_inc(se.wgt_sum, 1)
                    nc.vector.tensor_tensor(ctx_in[:, 0, :, :], ctx_in[:, 0, :, :], ctx_in[:, 1, :, :], ALU.add).then_inc(se.ctx_sum, 1)
                    wait(dve, se.wgt_sum, c + 1)
                    nc.vector.reciprocal(wgt_in[:, 0, :, :], wgt_in[:, 0, :, :]).then_inc(se.wgt_inv, 1)
                    wait(dve, se.wgt_inv, c + 1)
                    wait(dve, se.ctx_sum, c + 1)
                    wait(dve, se.o_ps, c * 2)
                    nc.vector.tensor_tensor(proj_in[:, :, :], ctx_in[:, 0, :, :], wgt_in[:, 0, :, :], ALU.mult).then_inc(se.ctx_n, 1)

                def add_attention(c):
                    for j in range(2):
                        wait(dve, se.o_ps, c * 2 + j + 1)
                        nc.vector.tensor_tensor(x_tiles(c, 2 * j, 2), f.acc[:, j, :], x_tiles(c, 2 * j, 2), ALU.add).then_inc(se.x2, 1)
                    wait(dve, se.x2, c * 2 + 2)
                    dve.sem_inc(se.gate, 1)
                    dve_ln_stats(ln3, c)
                    if isinstance(c, int) and c == 0:
                        normalize(1)
                    dve_ln_finish(ln3, c, f.sem.t_ps)

                normalize(0)
                dve.wait_ge(sb.bo_add, NCH * TPC)
                add_attention(0)
                dve_x(f, 0)
                dve_hidden(f, 0, range(HT), 0)

                def chunk(c, last=False, norm=True):
                    dve_hidden(f, c, range(0, 2), 1)
                    if not last:
                        add_attention(c + 1)
                    dve_hidden(f, c, range(2, 4), 1)
                    if norm:
                        normalize(c + 2)
                    dve_hidden(f, c, range(4, 6), 1)
                    if not last:
                        dve_x(f, c + 1)
                    dve_hidden(f, c, range(6, HT), 1)
                    dve_residual(f, c)
                    if not last:
                        dve_hidden(f, c + 1, range(HT), 0)

                chunk(0)
                with dve.Fori(1, NCH - 2) as c:
                    chunk(c)
                chunk(NCH - 2, norm=False)
                chunk(NCH - 1, last=True, norm=False)

            @block.scalar
            def _(act):
                act_x(f, 0)
                act_hidden(f, 0, range(HT), 0)

                def chunk(c, last=False):
                    act_hidden(f, c, range(0, 2), 1)
                    if not last:
                        act_ln_sqrt(ln3, c + 1)
                    act_hidden(f, c, range(2, 6), 1)
                    if not last:
                        act_x(f, c + 1)
                    act_hidden(f, c, range(6, HT), 1)
                    if not last:
                        act_hidden(f, c + 1, range(HT), 0)

                chunk(0)
                with act.Fori(1, NCH - 1) as c:
                    chunk(c)
                chunk(NCH - 1, last=True)

            @block.tensor
            def _(pe):
                def turn(c):
                    wait(pe, ln3.sem.xn, c + 1)
                    wait(pe, f.sem.xl, c)
                    pe_transpose(ln3, f.tr, f.sem.t_ps)

                def l0_free(c):
                    def free(m):
                        if m >= 4:
                            wait(pe, f.sem.l0_lo, c * HT + m - 3)
                        elif not (isinstance(c, int) and c == 0):
                            wait(pe, f.sem.l1_lo, (c - 1) * HT + 5 + m)
                        elif m < ST_BANKS:
                            wait(pe, sb.exp_done, BODIES * EXPS)
                        else:
                            wait(pe, sb.ctx_done, BATCH * PAIRS * QCH)
                    return free

                def l1_free(c):
                    def free(m):
                        if m == 0:
                            wait(pe, f.sem.l0_lo, c * HT + 5)
                        elif m >= 4:
                            wait(pe, f.sem.l1_lo, c * HT + m - 3)
                    return free

                def chunk(c, first=False, last=False):
                    pe_l1(f, c, range(0, 2), l1_free(c))
                    if not last:
                        pe_out_proj(pe, c + 1, lambda j: wait(pe, se.x2, j + 1) if first else wait(pe, f.sem.res, c * 2 + j - 1))
                    pe_l1(f, c, range(2, 6), l1_free(c))
                    if not last:
                        turn(c + 1)
                    pe_l1(f, c, range(6, HT), l1_free(c))
                    pe_l2(f, c, lambda j: wait(pe, f.sem.res, c * 2 + j - 1) if last else wait(pe, se.x2, c * 2 + j + 3))
                    if not last:
                        pe_l0(f, c + 1, l0_free(c + 1))

                turn(0)
                pe_l0(f, 0, l0_free(0))
                chunk(0, first=True)
                with pe.Fori(1, NCH - 1) as c:
                    chunk(c)
                chunk(NCH - 1, last=True)


_INS = ["L0_attn_x", "L0_attn_w_q", "L0_attn_w_k", "L0_attn_w_v", "L0_attn_w_o", "L0_attn_b_o",
        "L0_ffn_k0", "L0_ffn_k1", "L0_ffn_k2", "L0_ffn_s0", "L0_ffn_s1", "L0_ffn_s2"]


def kernel(**inputs):
    import numpy as np
    import concourse.bacc as bacc
    from concourse.bass_utils import run_bass_kernel_spmd

    nc = bacc.Bacc("TRN2", target_bir_lowering=False, num_devices=1)
    arrays, args = {}, []
    for name in _INS:
        a = np.ascontiguousarray(inputs[name])
        if a.ndim == 0:
            a = a.reshape(1)
        arrays[name] = a
        args.append(nc.dram_tensor(name, a.shape, U8 if a.dtype == np.bool_ else F32, kind="ExternalInput").ap())
    shape = arrays["L0_attn_x"].shape
    args.append(nc.dram_tensor("out", shape, F32, kind="ExternalOutput").ap())
    build(nc, *args)
    result = run_bass_kernel_spmd(nc, [arrays], core_ids=[0])
    return result.results[0]["out"]
```
